# Optimizing a Trainium2 kernel written in Bass

```python
import numpy as np
import jax
import jax.numpy as jnp

def _softmax(x, axis=-1):
    return jax.nn.softmax(x, axis=axis)

def _gelu(x):
    return jax.nn.gelu(x, approximate=True)

def _silu(x):
    return jax.nn.silu(x)

def _sigmoid(x):
    return jax.nn.sigmoid(x)

def _layernorm(x, axis=-1, eps=1e-05):
    m = jnp.mean(x, axis=axis, keepdims=True)
    v = jnp.var(x, axis=axis, keepdims=True)
    return (x - m) / jnp.sqrt(v + eps)

def _scatter_add(tgt, idx, src, axis=0):
    return tgt.at[idx].add(src)

def _segment_sum(src, seg, n):
    return jax.ops.segment_sum(src, seg, n)
kernel_name = 'mk_adj_preln_d4_adj_r2_86c03c'

def setup_inputs(seed: int=0):
    np.random.seed(seed)
    _w = jnp.asarray

    def _rec_inputs():
        import jax
        import jax.numpy as jnp
        _gk = jax.random.key(seed)
        x = 0.5001 + 0.2887 * jax.random.normal(jax.random.fold_in(_gk, 1), (4096, 64), jnp.float32)
        _a = jax.random.bernoulli(jax.random.fold_in(_gk, 2), 0.000976562, (4096, 4096))
        _a = jnp.logical_or(_a, jnp.eye(4096, dtype=bool))
        _af = _a.astype(jnp.float32)
        _af = _af * jax.random.uniform(jax.random.fold_in(_gk, 3), (4096, 4096), jnp.float32, 0.05, 1)
        adj = _af
        return (x, adj)
    x, adj = _rec_inputs()

    def _L0_gnn_setup():
        import jax, jax.numpy as jnp
        import numpy as np
        N = 5000
        DIM = 64
        F_CONST = 1.0
        B_CONST = 0.1
        R_CONST = 0.01
        key = jax.random.key(seed)
        k1, k2 = jax.random.split(key)
        t = jnp.zeros((1,), dtype=jnp.float32)
        x = jax.random.uniform(k1, (N, DIM), dtype=jnp.float32)
        A = jax.random.uniform(k2, (N, N), dtype=jnp.float32)
        return {'t': t, 'x': x, 'A': A}
    _L0_gnn_all = _L0_gnn_setup()
    _L0_gnn_in = {k: v for k, v in _L0_gnn_all.items() if k in ('t',)}
    del _L0_gnn_all

    def _L1_gnn_setup():
        import jax, jax.numpy as jnp
        import numpy as np
        N = 8192
        IN_C = 64
        OUT_C = 64
        key = jax.random.key(seed)
        k1, k2, k3 = jax.random.split(key, 3)
        x = jax.random.normal(k1, (N, IN_C), dtype=jnp.float32)
        adj = jax.random.uniform(k2, (N, N), dtype=jnp.float32)
        scale = jnp.sqrt(6.0 / (IN_C + OUT_C))
        weight = jax.random.uniform(k3, (IN_C, OUT_C), dtype=jnp.float32, minval=-scale, maxval=scale)
        return {'x': x, 'adj': adj, 'weight': weight}
    _L1_gnn_all = _L1_gnn_setup()
    _L1_gnn_in = {k: v for k, v in _L1_gnn_all.items() if k in ('weight',)}
    del _L1_gnn_all

    def _L2_gnn_setup():
        import jax, jax.numpy as jnp
        import numpy as np
        N = 8192
        F_IN = 64
        F_OUT = 64
        key = jax.random.key(seed)
        k1, k2, k3 = jax.random.split(key, 3)
        inp = jax.random.normal(k1, (N, F_IN), dtype=jnp.float32)
        adj = jax.random.uniform(k2, (N, N), dtype=jnp.float32)
        limit = np.sqrt(6.0 / (F_IN + F_OUT)).astype(np.float32)
        W = jax.random.uniform(k3, (F_IN, F_OUT), dtype=jnp.float32, minval=-limit, maxval=limit)
        b = jnp.zeros((F_OUT,), dtype=jnp.float32)
        return {'input': inp, 'adj': adj, 'W': W, 'b': b}
    _L2_gnn_all = _L2_gnn_setup()
    _L2_gnn_in = {k: v for k, v in _L2_gnn_all.items() if k in ('W', 'b')}
    del _L2_gnn_all

    def _L3_gnn_setup():
        import jax, jax.numpy as jnp
        import numpy as np
        N = 4096
        H = 64
        ALPHA = 0.2
        NEG_INF = -9000000000000000.0

        def gru_cell(x, h, w_ih, w_hh, b_ih, b_hh):
            gi = x @ w_ih.T + b_ih
            gh = h @ w_hh.T + b_hh
            ir, iz, inn = jnp.split(gi, 3, axis=1)
            hr, hz, hn = jnp.split(gh, 3, axis=1)
            r = jax.nn.sigmoid(ir + hr)
            z = jax.nn.sigmoid(iz + hz)
            n = jnp.tanh(inn + r * hn)
            return (1.0 - z) * n + z * h

        def gat(h, node_adj, edge_adj, W, a):
            hw = h @ W
            h_plus = (node_adj > 0).astype(hw.dtype) @ hw
            h_minus = (node_adj < 0).astype(hw.dtype) @ hw
            e_plus = jax.nn.leaky_relu(jnp.concatenate([h_plus, h_minus], axis=1) @ a, ALPHA)
            e_minus = jax.nn.leaky_relu(jnp.concatenate([h_minus, h_plus], axis=1) @ a, ALPHA)
            att = jnp.where(edge_adj > 0, e_plus, NEG_INF)
            att = jnp.where(edge_adj < 0, e_minus, att)
            att = jax.nn.softmax(att, axis=1)
            return att * edge_adj @ hw
        key = jax.random.key(seed)
        ks = jax.random.split(key, 12)
        f32 = jnp.float32
        inp = {'h': jax.random.normal(ks[0], (N, H), f32), 'node_adj': jax.random.normal(ks[1], (N, N), f32), 'edge_adj': jax.random.normal(ks[2], (N, N), f32), 'W_gat': jax.random.normal(ks[3], (H, H), f32) * (1.414 * np.sqrt(6.0 / (2 * H))), 'a_gat': jax.random.normal(ks[4], (2 * H, 1), f32) * (1.414 * np.sqrt(6.0 / (2 * H + 1))), 'w_ih_e': jax.random.normal(ks[5], (3 * H, 2 * H), f32) * 0.01, 'w_hh_e': jax.random.normal(ks[6], (3 * H, H), f32) * 0.01, 'b_ih_e': jnp.zeros((3 * H,), f32), 'b_hh_e': jnp.zeros((3 * H,), f32), 'w_ih_n': jax.random.normal(ks[7], (3 * H, H), f32) * 0.01, 'w_hh_n': jax.random.normal(ks[8], (3 * H, H), f32) * 0.01, 'b_ih_n': jnp.zeros((3 * H,), f32), 'b_hh_n': jnp.zeros((3 * H,), f32)}
        return inp
    _L3_gnn_all = _L3_gnn_setup()
    _L3_gnn_in = {k: v for k, v in _L3_gnn_all.items() if k in ('W_gat', 'a_gat', 'w_ih_e', 'w_hh_e', 'b_ih_e', 'b_hh_e', 'w_ih_n', 'w_hh_n', 'b_ih_n', 'b_hh_n')}
    del _L3_gnn_all
    return {'x': x, 'adj': adj, 'L0_gnn_t': _L0_gnn_in['t'], 'L1_gnn_weight': _L1_gnn_in['weight'], 'L2_gnn_W': _L2_gnn_in['W'], 'L2_gnn_b': _L2_gnn_in['b'], 'L3_gnn_W_gat': _L3_gnn_in['W_gat'], 'L3_gnn_a_gat': _L3_gnn_in['a_gat'], 'L3_gnn_w_ih_e': _L3_gnn_in['w_ih_e'], 'L3_gnn_w_hh_e': _L3_gnn_in['w_hh_e'], 'L3_gnn_b_ih_e': _L3_gnn_in['b_ih_e'], 'L3_gnn_b_hh_e': _L3_gnn_in['b_hh_e'], 'L3_gnn_w_ih_n': _L3_gnn_in['w_ih_n'], 'L3_gnn_w_hh_n': _L3_gnn_in['w_hh_n'], 'L3_gnn_b_ih_n': _L3_gnn_in['b_ih_n'], 'L3_gnn_b_hh_n': _L3_gnn_in['b_hh_n']}

def reference(x, adj, L0_gnn_t, L1_gnn_weight, L2_gnn_W, L2_gnn_b, L3_gnn_W_gat, L3_gnn_a_gat, L3_gnn_w_ih_e, L3_gnn_w_hh_e, L3_gnn_b_ih_e, L3_gnn_b_hh_e, L3_gnn_w_ih_n, L3_gnn_w_hh_n, L3_gnn_b_ih_n, L3_gnn_b_hh_n):
    import jax
    import jax.numpy as jnp

    def _L0_gnn_ref(t, x, A):
        import jax, jax.numpy as jnp
        import numpy as np
        N = 5000
        DIM = 64
        F_CONST = 1.0
        B_CONST = 0.1
        R_CONST = 0.01
        Ax = A @ x
        outer = R_CONST * jnp.sum(x * Ax, axis=1, keepdims=True)
        return F_CONST - B_CONST * x - outer

    def _L1_gnn_ref(x, adj, weight):
        import jax, jax.numpy as jnp
        import numpy as np
        N = 8192
        IN_C = 64
        OUT_C = 64
        agg = adj @ x
        return agg @ weight

    def _L2_gnn_ref(input, adj, W, b):
        import jax, jax.numpy as jnp
        import numpy as np
        N = 8192
        F_IN = 64
        F_OUT = 64
        h = input @ W
        out = adj @ h + b
        return out

    def _L3_gnn_ref(h, node_adj, edge_adj, W_gat, a_gat, w_ih_e, w_hh_e, b_ih_e, b_hh_e, w_ih_n, w_hh_n, b_ih_n, b_hh_n):
        import jax, jax.numpy as jnp
        import numpy as np
        N = 4096
        H = 64
        ALPHA = 0.2
        NEG_INF = -9000000000000000.0

        def gru_cell(x, h, w_ih, w_hh, b_ih, b_hh):
            gi = x @ w_ih.T + b_ih
            gh = h @ w_hh.T + b_hh
            ir, iz, inn = jnp.split(gi, 3, axis=1)
            hr, hz, hn = jnp.split(gh, 3, axis=1)
            r = jax.nn.sigmoid(ir + hr)
            z = jax.nn.sigmoid(iz + hz)
            n = jnp.tanh(inn + r * hn)
            return (1.0 - z) * n + z * h

        def gat(h, node_adj, edge_adj, W, a):
            hw = h @ W
            h_plus = (node_adj > 0).astype(hw.dtype) @ hw
            h_minus = (node_adj < 0).astype(hw.dtype) @ hw
            e_plus = jax.nn.leaky_relu(jnp.concatenate([h_plus, h_minus], axis=1) @ a, ALPHA)
            e_minus = jax.nn.leaky_relu(jnp.concatenate([h_minus, h_plus], axis=1) @ a, ALPHA)
            att = jnp.where(edge_adj > 0, e_plus, NEG_INF)
            att = jnp.where(edge_adj < 0, e_minus, att)
            att = jax.nn.softmax(att, axis=1)
            return att * edge_adj @ hw
        d_node = jnp.diag(node_adj)
        d_edge = jnp.diag(edge_adj)
        A_node = node_adj - jnp.diag(d_node)
        A_edge = edge_adj - jnp.diag(d_edge)
        node_support = jnp.concatenate([(A_node > 0).astype(h.dtype) @ h, (A_node < 0).astype(h.dtype) @ h], axis=1)
        edge_output = gru_cell(node_support, h, w_ih_e, w_hh_e, b_ih_e, b_hh_e)
        edge_support = gat(h, A_node, A_edge, W_gat, a_gat)
        node_output = gru_cell(edge_support, h, w_ih_n, w_hh_n, b_ih_n, b_hh_n)
        return d_edge[:, None] * edge_output + d_node[:, None] * node_output
    h = jnp.maximum(_layernorm(x, axis=-1), 0.0)
    x = x + _L0_gnn_ref(L0_gnn_t, h, adj)
    h = jnp.maximum(_layernorm(x, axis=-1), 0.0)
    x = x + _L1_gnn_ref(h, adj, L1_gnn_weight)
    h = jnp.maximum(_layernorm(x, axis=-1), 0.0)
    x = x + _L2_gnn_ref(h, adj, L2_gnn_W, L2_gnn_b)
    h = jnp.maximum(_layernorm(x, axis=-1), 0.0)
    x = x + _L3_gnn_ref(h, adj, adj, L3_gnn_W_gat, L3_gnn_a_gat, L3_gnn_w_ih_e, L3_gnn_w_hh_e, L3_gnn_b_ih_e, L3_gnn_b_hh_e, L3_gnn_w_ih_n, L3_gnn_w_hh_n, L3_gnn_b_ih_n, L3_gnn_b_hh_n)
    return x

_drawn_inputs = setup_inputs


def setup_inputs(seed=0):
    import zlib

    import numpy as np

    out = dict(_drawn_inputs(seed))
    spreads = {'L2_gnn_b': (0.0, 0.1),
     'L3_gnn_b_ih_e': (0.0, 0.777),
     'L3_gnn_b_hh_e': (0.0, 0.8),
     'L3_gnn_b_ih_n': (0.0, 0.707),
     'L3_gnn_b_hh_n': (0.0, 2.0)}
    factors = {'L3_gnn_W_gat': 8.0,
     'L3_gnn_w_ih_e': 3.056,
     'L3_gnn_w_hh_e': 8.0,
     'L3_gnn_w_ih_n': 7.02,
     'L3_gnn_w_hh_n': 32.527}
    for name, (base, spread) in spreads.items():
        noise = np.random.default_rng([zlib.crc32(name.encode()), seed]).standard_normal(out[name].shape)
        drawn = base * np.exp(spread * noise) if base else spread * noise
        out[name] = jnp.asarray(drawn.astype(out[name].dtype))
    for name, factor in factors.items():
        out[name] = (out[name] * factor).astype(out[name].dtype)
    return out
```

```python
from contextlib import ExitStack

import numpy as np

import concourse.bass as bass
from concourse import mybir

F32 = mybir.dt.float32
F32R = mybir.dt.float32r
BF16 = mybir.dt.bfloat16
ALU = mybir.AluOpType
ACT = mybir.ActivationFunctionType
AX_X = mybir.AxisListType.X

P = 128
EPS = 1e-5
F_CONST, B_CONST, R_CONST = 1.0, 0.1, 0.01
ALPHA = 0.2
NEG_INF = -9000000000000000.0
ABSENT = -3.0e38


def gnn_stack(nc, x, adj, bd1, w2s, b2, wgat_t2, a2, wih_n_t, b_in, we1, we2, haug, out):
    N, D = x.shape
    RT = N // P
    IT = 4
    BLK = IT * P
    NB = N // BLK
    NQ = 4
    QC = N // NQ
    NT = N // P
    NS = NT // 2
    SQ = NS // NQ
    G3 = 3 * D
    EV = G3 + 2

    adj_blocks = adj.rearrange("(b t p) j -> b p t j", t=IT, p=P)
    x_rows = x.rearrange("(t p) d -> p t d", p=P)
    out_rows = out.rearrange("(b t p) d -> b p t d", t=IT, p=P)

    with ExitStack() as ctx:
        def sb(name, shape, dt=F32):
            return ctx.enter_context(nc.sbuf_tensor(name, shape, dt))

        def sem(name):
            return ctx.enter_context(nc.semaphore(name))

        PS = ctx.enter_context(nc.psum_tensor("PS", [P, 8, 512], F32))
        TURN, ACC_A, ACC_P, ACC_M, ACC_N, TAIL_G, TAIL_U = 0, 2, 3, 4, 5, 6, 7

        nat = sb("nat", [P, NQ, IT, QC])
        turned_sb = sb("turned_sb", [P, 4, BLK])
        pos = sb("pos", [P, 4, BLK], F32R)
        neg = sb("neg", [P, 4, BLK], F32R)
        low = sb("low", [P, 4, BLK])
        X = sb("X", [P, RT, D])
        H_buf = sb("H_buf", [P, RT * 2 * D])
        H01 = H_buf[:].rearrange("p (t d) -> p t d", t=RT)
        H3 = H_buf[:, 0:RT * D].rearrange("p (t d) -> p t d", t=RT)
        own = H_buf[:, RT * D:RT * D + 4 * BLK].rearrange("p (k n) -> p k n", k=4)
        H2 = sb("H2", [P, RT, D])
        H3HL = sb("H3HL", [P, RT, 2 * D], F32R)
        H3T = sb("H3T", [D, N])
        hT = sb("hT", [D + 2, BLK])
        saved = sb("saved", [P, 4, BLK])
        diag_sq = sb("diag_sq", [P, IT, P])
        ident = sb("ident", [P, P])
        ones = sb("ones", [P, D])
        dN = sb("dN", [P, RT])
        b2_sb = sb("b2_sb", [P, D])
        b_in_sb = sb("b_in_sb", [P, D])
        bd1_sb = sb("bd1_sb", [P, 2 * D])
        w2s_sb = sb("w2s_sb", [P, D])
        wg_sb = sb("wg_sb", [D, 2 * D])
        a2_sb = sb("a2_sb", [D, 2])
        wn_sb = sb("wn_sb", [D, G3])
        we1_sb = sb("we1_sb", [P, EV])
        we2_sb = sb("we2_sb", [P, EV])
        haug_sb = sb("haug_sb", [D + 2, 512])
        v2_sb = sb("v2_sb", [P, G3])
        eps_sb = sb("eps_sb", [P, 1])
        LG = 8
        xc = sb("xc", [P, LG, D])
        sq = sb("sq", [P, LG, D])
        st = sb("st", [P, 5, LG])
        hrow = sb("hrow", [P, IT, D])
        wrow = sb("wrow", [P, IT, D])
        sgn_blk = sb("sgn_blk", [P, IT, NQ])
        pos_blk = sb("pos_blk", [P, IT, NQ])
        sgn_n = sb("sgn_n", [P, RT])
        pos_n = sb("pos_n", [P, RT])
        junk_a = sb("junk_a", [P, QC], BF16)
        junk_v = sb("junk_v", [P, QC], BF16)
        dsign = sb("dsign", [P, 2, RT])
        cnt = sb("cnt", [P, RT, 3])
        pen = sb("pen", [P, RT, 2])
        below_p = sb("below_p", [P, 1])
        any_below = sb("any_below", [1, 1], mybir.dt.int32)
        V = sb("V", [P, 3])
        E = sb("E", [P, 3])
        sm = sb("sm", [P, 8])
        pr = sb("pr", [P, 2])
        T1 = sb("T1", [P, G3])
        TH = sb("TH", [P, 2, 2 * D])
        RH = sb("RH", [P, 2, D])
        PN = sb("PN", [P, 2, D])
        NN = sb("NN", [P, 2, D])
        OO = sb("OO", [P, 2, D])

        x_loaded = [sem(f"x_loaded{i}") for i in range(RT // LG)]
        bd1_loaded = sem("bd1_loaded")
        w_loaded = sem("w_loaded")
        nat_loaded = [sem(f"nat_loaded{i}") for i in range(NQ)]
        ident_made = sem("ident_made")
        consts_made = sem("consts_made")
        prod_made = sem("prod_made")
        prod_saved = sem("prod_saved")
        turned = sem("turned")
        even_out = sem("even_out")
        odd_out = sem("odd_out")
        signs_done = sem("signs_done")
        above_done = sem("above_done")
        counts_taken = sem("counts_taken")
        masked = sem("masked")
        acc_full = sem("acc_full")
        acc_saved = sem("acc_saved")
        var_ready = sem("var_ready")
        std_ready = sem("std_ready")
        h_ready = sem("h_ready")
        tail_ready = sem("tail_ready")
        rows_ready = sem("rows_ready")
        hT_made = sem("hT_made")
        hT_saved = sem("hT_saved")
        hT_block = sem("hT_block")
        diag_made = sem("diag_made")
        diag_wide = sem("diag_wide")
        v_ready = sem("v_ready")
        e_ready = sem("e_ready")
        p_ready = sem("p_ready")
        t_ready = sem("t_ready")
        g_ready = sem("g_ready")
        r_ready = sem("r_ready")
        pn_ready = sem("pn_ready")
        n_ready = sem("n_ready")
        out_ready = sem("out_ready")
        stored = sem("stored")
        below_counted = sem("below_counted")
        below_summed = sem("below_summed")
        any_below_ready = sem("any_below_ready")

        block = ctx.enter_context(nc.Block())

        def over_blocks(eng, body, last_apart):
            body(0, True, False)
            with eng.Fori(1, NB - 1 if last_apart else NB) as b:
                body(b, False, False)
            if last_apart:
                body(NB - 1, False, True)

        def either_way(eng, pass3):
            eng.wait_ge(any_below_ready, 1)
            some = eng.value_load(any_below[0:1, 0:1], min_val=0, max_val=1)
            with eng.If(some != 0):
                pass3(True)
            with eng.Else():
                pass3(False)

        def even_count(p, b, c):
            return (p * NB + b) * NS + c // 2 + 1 if p < 2 else 2 * NB * NS + b * NT + c + 1

        def odd_count(p, b, c):
            return (p * NB + b) * NS + c // 2 + 1 if p < 2 else 2 * NB * NS

        @block.sync
        def _(sp):
            for g in range(RT // LG):
                sp.dma_start(X[:, g * LG:(g + 1) * LG, :], x_rows[:, g * LG:(g + 1) * LG, :]).then_inc(x_loaded[g], 16)

            def load_block(p, b, first):
                for q in range(NQ):
                    if not (p == 0 and first):
                        sp.wait_ge(turned, (p * NB + b - 1) * NT + (q + 1) * 2 * SQ + (4 if p == 0 or p == 1 and first else 0))
                    sp.dma_start(nat[:, q, :, :], adj_blocks[b, :, :, q * QC:(q + 1) * QC]).then_inc(nat_loaded[q], 16)

            sp.dma_start(bd1_sb[:], bd1).then_inc(bd1_loaded, 16)
            for p in range(3):
                load_block(p, 0, True)
                with sp.Fori(1, NB) as b:
                    load_block(p, b, False)

        @block.gpsimd
        def _(pool):
            nc.gpsimd.memset(ident[:], 0.0)
            pool.drain()
            nc.gpsimd.affine_select(out=ident[:], in_=ident[:], compare_op=ALU.not_equal, fill=1.0, base=0,
                                    pattern=[[-1, P]], channel_multiplier=1).then_inc(ident_made, 1)
            with nc.allow_non_contiguous_dma(reason="the diagonal"):
                loads = [(w2s_sb, w2s), (wg_sb, wgat_t2), (a2_sb, a2), (wn_sb, wih_n_t),
                         (we1_sb, we1), (we2_sb, we2), (haug_sb, haug),
                         (b2_sb, b2.to_broadcast([P, D])), (b_in_sb, b_in.to_broadcast([P, D]))]
                for dst, src in loads:
                    pool.dma_start(dst[:, 0:src.shape[1]], src).then_inc(w_loaded, 16)
                diag = bass.AP(tensor=adj.tensor, offset=adj.offset, ap=[[N + 1, P], [P * (N + 1), RT], [1, 1]])
                pool.dma_start(dN[:].rearrange("p (t o) -> p t o", o=1), diag).then_inc(w_loaded, 16)
            with pool.Fori(0, NB) as b:
                pool.wait_ge(out_ready, b * IT + IT)
                pool.dma_start(out_rows[b], X[:, bass.ds(b * IT, IT), :]).then_inc(stored, 16)
            pool.wait_ge(stored, 16 * NB)

        N_LOADS = 10

        @block.tensor
        def _(pe):
            def turn(p, b, s):
                if s % SQ == 0:
                    pe.wait_ge(nat_loaded[(s // SQ) % NQ], 16 * (p * NB + b + s // NS + 1))
                for c in (2 * s, 2 * s + 1):
                    q, k = (c // (2 * SQ)) % NQ, c % (2 * SQ)
                    for it in range(IT):
                        ins = pe.transpose(PS[:, TURN + c % 2, it * P:(it + 1) * P],
                                           nat[:, q, it, k * P:(k + 1) * P], ident[:])
                    ins.then_inc(turned, 1)

            def products(p, b, s, below):
                for c in (2 * s, 2 * s + 1):
                    A = turned_sb[:, c % 4, :]
                    first, last = c == 0, c == NT - 1
                    if p == 0:
                        ins = pe.matmul(PS[:, ACC_A, :], H01[:, c, :], A, start=first, stop=last)
                    else:
                        h = (H2, H3)[p - 1][:, c, :]
                        half = slice(D * (c % 2), D * (c % 2) + D)
                        ins = pe.matmul(PS[half, ACC_A, :], h, A, start=c < 2, stop=c >= NT - 2)
                if p == 2:
                    for c in (2 * s, 2 * s + 1) if below else ():
                        half = slice(D * (c % 2), D * (c % 2) + D)
                        pe.matmul(PS[half, ACC_N, :], H3[:, c, :], low[:, c % 4, :], start=c < 2, stop=c >= NT - 2)
                    for c in (2 * s, 2 * s + 1):
                        first, last = c == 0, c == NT - 1
                        ins = pe.matmul(PS[:, ACC_P, :], H3HL[:, c, :], pos[:, c % 4, :], start=first, stop=last)
                    for c in (2 * s, 2 * s + 1) if below else ():
                        first, last = c == 0, c == NT - 1
                        ins = pe.matmul(PS[:, ACC_M, :], H3HL[:, c, :], neg[:, c % 4, :], start=first, stop=last)
                if s == NS - 1:
                    ins.then_inc(acc_full, 1)

            def tail12(p, b):
                pe.wait_ge(acc_saved, p * NB + b + 1)
                for it in range(IT):
                    rows = saved[:, 0, it * P:(it + 1) * P]
                    w, n = ((bd1_sb, 2 * D), (w2s_sb, D))[p]
                    ins = pe.matmul(PS[:, TAIL_G, it * n:(it + 1) * n], rows, w[:], start=True, stop=True)
                ins.then_inc(tail_ready, 1)

            def turn_h3(b):
                for it in range(IT):
                    ins = pe.transpose(PS[0:D, TAIL_U, it * P:(it + 1) * P], hrow[:, it, :], ident[:])
                ins.then_inc(hT_made, 1)

            def tail3(b, it, below):
                cols = slice(it * P, (it + 1) * P)
                if it == 0:
                    pe.wait_ge(acc_saved, 2 * NB + b + 1)
                    pe.wait_ge(hT_block, b + 1)
                else:
                    pe.wait_ge(pn_ready, b * IT + it)
                pe.matmul(PS[:, TAIL_G, :], hT[:, cols], haug_sb[:], start=True, stop=False, skip_group_check=True)
                pe.matmul(PS[:, TAIL_G, D:D + EV], saved[:, 1, cols], we1_sb[:], start=False, stop=not below, skip_group_check=True)
                if below:
                    pe.matmul(PS[:, TAIL_G, D:D + EV], saved[:, 2, cols], we2_sb[:], start=False, stop=True, skip_group_check=True)
                    pe.matmul(PS[:, TAIL_U, G3:2 * G3], saved[:, 3, cols], v2_sb[:], start=True, stop=True)
                pe.matmul(PS[:, TAIL_U, 0:G3], saved[:, 0, cols], v2_sb[:], start=True, stop=True).then_inc(tail_ready, 1)

            def widen_diag(b):
                pe.wait_ge(diag_made, b + 1)
                if not (isinstance(b, int) and b == 0):
                    pe.wait_ge(pn_ready, b * IT)
                pe.matmul(PS[0:D, TAIL_U, :], ones[:], diag_sq[:].rearrange("p t q -> p (t q)"),
                          start=True, stop=True).then_inc(diag_wide, 1)

            def pass_block(p, below=False):
                def body(b, first, last):
                    for s in range(NS):
                        pe.wait_ge(even_out, even_count(p, b, 2 * s + (p == 2)))
                        if p < 2:
                            pe.wait_ge(odd_out, odd_count(p, b, 2 * s))
                        if not (last and s == NS - 1):
                            turn(p, b, s + 1)
                        if s == 0 and not first:
                            pe.wait_ge(acc_saved, p * NB + b)
                        if first and p == 0 and (2 * s) % LG == 0:
                            pe.wait_ge(h_ready, 2 * s // LG + 1)
                        if first and p > 0 and s == 0:
                            pe.wait_ge(rows_ready, p * NB)
                        if p == 2:
                            pe.wait_ge(masked, b * NS + s + 1)
                        if not first and p == 1 and s == 8:
                            pe.wait_ge(rows_ready, NB + b)
                        products(p, b, s, below)
                        if not first and p < 2 and s == 2:
                            tail12(p, b - 1)
                        if not first and p == 1 and s == 8:
                            turn_h3(b - 1)
                        if not first and p == 2 and s in (1, 4, 7, 10):
                            tail3(b - 1, (s - 1) // 3, below)
                        if p == 2 and s == 14:
                            widen_diag(b)
                return body

            pe.wait_ge(ident_made, 1)
            pe.wait_ge(consts_made, 1)
            turn(0, 0, 0)
            pe.wait_ge(bd1_loaded, 16)
            over_blocks(pe, pass_block(0), False)
            pe.wait_ge(w_loaded, 16 * N_LOADS)
            pe.matmul(PS[:, TAIL_U, 0:2], wg_sb[:], a2_sb[:], start=True, stop=True)
            pe.matmul(PS[:, TAIL_U, 2:2 + G3], wg_sb[:], wn_sb[:], start=True, stop=True).then_inc(prod_made, 1)
            tail12(0, NB - 1)
            pe.wait_ge(below_counted, 1)
            pe.matmul(PS[0:1, TAIL_U, 0:1], below_p[:], ones[:, 0:1], start=True, stop=True).then_inc(below_summed, 1)
            over_blocks(pe, pass_block(1), False)
            tail12(1, NB - 1)
            pe.wait_ge(rows_ready, 2 * NB)
            turn_h3(NB - 1)
            pe.wait_ge(hT_saved, NB)

            def pass3(below):
                over_blocks(pe, pass_block(2, below), True)
                for it in range(IT):
                    tail3(NB - 1, it, below)

            either_way(pe, pass3)

        @block.scalar
        def _(act):
            def out_even(p, b, s):
                for c in (2 * s, 2 * s + 1) if p == 2 else (2 * s,):
                    act.wait_ge(turned, (p * NB + b) * NT + c + 1)
                    nc.scalar.copy(turned_sb[:, c % 4, :], PS[:, TURN + c % 2, :]).then_inc(even_out, 1)

            def count_signs(b, s, first):
                q, it = s // SQ, s % SQ
                act.drain()
                if s == 0 and not first:
                    act.wait_ge(counts_taken, b)
                nc.scalar.activation(junk_a[:], nat[:, q, it, :], ACT.Sign,
                                     accum_out=sgn_blk[:, it, q:q + 1]).then_inc(signs_done, 1)

            def save(p, b):
                act.wait_ge(acc_full, p * NB + b + 1)
                nc.scalar.copy(saved[:, 0, :], PS[:, ACC_A, :]).then_inc(acc_saved, 1)

            def deviations(n_before, tiles):
                act.wait_ge(var_ready, n_before + 1)
                nc.scalar.activation(st[:, 3, 0:tiles], st[:, 2, 0:tiles], ACT.Sqrt, bias=eps_sb[:],
                                     scale=1.0 / D).then_inc(std_ready, 1)

            def save_h3t(b):
                act.wait_ge(hT_made, b + 1)
                nc.scalar.copy(H3T[:, bass.ds(b * BLK, BLK)], PS[0:D, TAIL_U, :]).then_inc(hT_saved, 1)

            def fetch_hT(b):
                nc.scalar.copy(hT[0:D, :], H3T[:, bass.ds(b * BLK, BLK)]).then_inc(hT_block, 1)

            def a1(b, it):
                act.wait_ge(v_ready, b * IT + it + 1)
                nc.scalar.activation(E[:], V[:], ACT.Exp, bias=sm[:, 1:2])
                nc.scalar.activation(TH[:, 0, :], PS[:, TAIL_G, D:3 * D], ACT.Tanh, scale=0.5).then_inc(e_ready, 1)

            def a2_(b, it):
                act.wait_ge(p_ready, b * IT + it + 1)
                nc.scalar.activation(T1[:], PS[:, TAIL_U, 0:G3], ACT.Copy, scale=pr[:, 0:1]).then_inc(t_ready, 1)

            def a3(b, it):
                act.wait_ge(g_ready, b * IT + it + 1)
                nc.scalar.activation(TH[:, 1, :], T1[:, 0:2 * D], ACT.Tanh, scale=0.5).then_inc(r_ready, 1)

            def a4(b, it):
                act.wait_ge(pn_ready, b * IT + it + 1)
                nc.scalar.activation(NN[:], PN[:], ACT.Tanh).then_inc(n_ready, 1)

            def pass_block(p, below=False):
                def body(b, first, last):
                    for s in range(NS):
                        out_even(p, b, s)
                        if not first and s == 0 and p < 2:
                            save(p, b - 1)
                        if p == 0 and first and s // SQ + 1 < RT // LG and s % 2 == 0:
                            deviations(2 * (s // SQ + 1) + s % SQ // 2, LG)
                        if p == 0:
                            count_signs(b, s, first)
                        if not first and p < 2 and s == 5:
                            deviations(2 * (RT // LG) + p * NB + b - 1, IT)
                        if not first and p == 1 and s == 10:
                            save_h3t(b - 1)
                        if p == 2:
                            if not first:
                                t, k = divmod(s - 2, 3)
                                if 0 <= t < IT:
                                    if k == 0:
                                        a1(b - 1, t)
                                    if k == 1:
                                        a2_(b - 1, t)
                                        a3(b - 1, t)
                                    if k == 2:
                                        a4(b - 1, t)
                            if s == NS - 2:
                                fetch_hT(b)
                return body

            act.wait_ge(consts_made, 1)
            for n in range(2):
                deviations(n, LG)
            over_blocks(act, pass_block(0), False)
            save(0, NB - 1)
            deviations(2 * (RT // LG) + NB - 1, IT)
            over_blocks(act, pass_block(1), False)
            save(1, NB - 1)
            deviations(2 * (RT // LG) + 2 * NB - 1, IT)
            save_h3t(NB - 1)
            act.drain()
            over_blocks(act, pass_block(2), True)
            for t in range(IT):
                a1(NB - 1, t)
                a2_(NB - 1, t)
                a3(NB - 1, t)
                a4(NB - 1, t)

        @block.vector
        def _(dve):
            def wide(col, n):
                return col.rearrange("p (t o) -> p t o", o=1).to_broadcast([P, n, D])

            def norm_a(src, tiles):
                dve.tensor_reduce(st[:, 0, 0:tiles], src, AX_X, ALU.add)
                dve.drain()
                dve.tensor_scalar(st[:, 1, 0:tiles], st[:, 0, 0:tiles], 1.0 / D, None, ALU.mult)
                dve.drain()
                dve.tensor_tensor(xc[:, 0:tiles, :], src, wide(st[:, 1, 0:tiles], tiles), ALU.subtract)
                dve.drain()
                dve.tensor_tensor(sq[:, 0:tiles, :], xc[:, 0:tiles, :], xc[:, 0:tiles, :], ALU.mult)
                dve.drain()
                dve.tensor_reduce(st[:, 2, 0:tiles], sq[:, 0:tiles, :], AX_X, ALU.add).then_inc(var_ready, 1)

            def norm_b(dst, tiles, n_before):
                dve.wait_ge(std_ready, n_before + 1)
                dve.reciprocal(st[:, 4, 0:tiles], st[:, 3, 0:tiles])
                dve.drain()
                return dve.scalar_tensor_tensor(dst, xc[:, 0:tiles, :], 0.0, wide(st[:, 4, 0:tiles], tiles),
                                                ALU.max, ALU.mult)

            def out_odd(p, b, s):
                dve.wait_ge(turned, (p * NB + b) * NT + 2 * s + 2)
                dve.tensor_copy(turned_sb[:, (2 * s + 1) % 4, :], PS[:, TURN + 1, :]).then_inc(odd_out, 1)

            def count_above(b, s):
                q, it = s // SQ, s % SQ
                dve.drain()
                dve.tensor_scalar(junk_v[:], nat[:, q, it, :], 0.0, None, ALU.is_gt, ALU.add,
                                  accum_out=pos_blk[:, it, q:q + 1]).then_inc(above_done, 1)

            def take_counts(b):
                dve.drain()
                dve.wait_ge(signs_done, (b + 1) * NQ * IT)
                dve.tensor_reduce(sgn_n[:, bass.ds(b * IT, IT)], sgn_blk[:], AX_X, ALU.add)
                dve.tensor_reduce(pos_n[:, bass.ds(b * IT, IT)], pos_blk[:], AX_X, ALU.add).then_inc(counts_taken, 1)

            def tail1_a(b):
                t = bass.ds(b * IT, IT)
                dve.wait_ge(tail_ready, b + 1)
                Q = PS[:, TAIL_G, :].rearrange("p (t n) -> p t n", t=IT)
                dve.tensor_tensor(wrow[:], Q[:, :, 0:D], H01[:, t, 0:D], ALU.mult)
                dve.tensor_tensor(X[:, t, :], X[:, t, :], Q[:, :, D:2 * D], ALU.add)
                dve.drain()
                dve.tensor_reduce(sm[:, 0:IT], wrow[:], AX_X, ALU.add)
                dve.drain()
                dve.tensor_scalar(sm[:, 4:4 + IT], sm[:, 0:IT], -R_CONST, F_CONST, ALU.mult, ALU.add)
                dve.drain()
                dve.tensor_tensor(X[:, t, :], X[:, t, :], wide(sm[:, 4:4 + IT], IT), ALU.add)
                dve.drain()
                norm_a(X[:, t, :], IT)

            def tail1_b(b):
                norm_b(H2[:, bass.ds(b * IT, IT), :], IT, 2 * (RT // LG) + b).then_inc(rows_ready, 1)

            def tail2_a(b):
                t = bass.ds(b * IT, IT)
                dve.wait_ge(tail_ready, NB + b + 1)
                Q = PS[:, TAIL_G, 0:IT * D].rearrange("p (t n) -> p t n", t=IT)
                dve.tensor_tensor(X[:, t, :], X[:, t, :], b2_sb[:].rearrange("p (o d) -> p o d", o=1).to_broadcast([P, IT, D]), ALU.add)
                dve.drain()
                dve.tensor_tensor(X[:, t, :], X[:, t, :], Q, ALU.add)
                dve.drain()
                norm_a(X[:, t, :], IT)

            def tail2_b(b):
                t = bass.ds(b * IT, IT)
                norm_b(hrow[:], IT, 2 * (RT // LG) + NB + b)
                dve.drain()
                dve.tensor_copy(H3[:, t, :], hrow[:])
                dve.tensor_copy(H3HL[:, t, 0:D], hrow[:])
                dve.drain()
                dve.tensor_tensor(H3HL[:, t, D:2 * D], hrow[:], H3HL[:, t, 0:D].bitcast(F32), ALU.subtract).then_inc(rows_ready, 1)

            def mask(b, s, below):
                dve.wait_ge(even_out, even_count(2, b, 2 * s + 1))
                for c in (2 * s, 2 * s + 1):
                    A = turned_sb[:, c % 4, :]
                    ins = dve.tensor_scalar(pos[:, c % 4, :], A, 0.0, None, ALU.is_gt)
                for c in (2 * s, 2 * s + 1) if below else ():
                    A = turned_sb[:, c % 4, :]
                    dve.tensor_scalar(neg[:, c % 4, :], A, 0.0, None, ALU.is_lt)
                    dve.tensor_scalar(low[:, c % 4, :], A, 0.0, None, ALU.min)
                if below:
                    dve.drain()
                for c in (2 * s, 2 * s + 1) if below else ():
                    A = turned_sb[:, c % 4, :]
                    ins = dve.tensor_scalar(A, A, 0.0, None, ALU.max)
                ins.then_inc(masked, 1)

            def make_diag(b):
                dve.tensor_tensor(diag_sq[:], ident[:].rearrange("p (o q) -> p o q", o=1).to_broadcast([P, IT, P]),
                                  dN[:, bass.ds(b * IT, IT)].rearrange("p (t o) -> p t o", o=1).to_broadcast([P, IT, P]),
                                  ALU.mult).then_inc(diag_made, 1)

            def own_terms(b, below):
                dve.wait_ge(diag_wide, b + 1)
                dve.wait_ge(hT_block, b + 1)
                W = PS[0:D, TAIL_U, :]
                for k, op in ((0, ALU.max), (1, ALU.is_gt), (2, ALU.is_lt), (3, ALU.min))[:4 if below else 2]:
                    dve.scalar_tensor_tensor(own[0:D, k, :], W, 0.0, hT[0:D, :], op, ALU.mult)

            def save3(b, below):
                dve.drain()
                dve.wait_ge(acc_full, 2 * NB + b + 1)
                for k, bank in enumerate((ACC_A, ACC_P, ACC_M, ACC_N)[:4 if below else 2]):
                    ins = dve.tensor_tensor(saved[:, k, :], PS[:, bank, :], own[:, k, :], ALU.subtract)
                ins.then_inc(acc_saved, 1)

            def d1(b, it):
                t = b * IT + it
                dve.wait_ge(tail_ready, 2 * NB + t + 1)
                dve.tensor_scalar(V[:, 0:2], PS[:, TAIL_G, 4 * D:4 * D + 2], ALPHA, None, ALU.mult)
                dve.drain()
                dve.tensor_tensor(V[:, 0:2], V[:, 0:2], PS[:, TAIL_G, 4 * D:4 * D + 2], ALU.max)
                dve.drain()
                dve.tensor_tensor(V[:, 0:2], V[:, 0:2], pen[:, bass.ds(t, 1), :].rearrange("p o k -> p (o k)"), ALU.add)
                dve.drain()
                dve.tensor_reduce(sm[:, 0:1], V[:], AX_X, ALU.max)
                dve.drain()
                dve.tensor_scalar(sm[:, 1:2], sm[:, 0:1], -1.0, None, ALU.mult).then_inc(v_ready, 1)

            def d2(b, it):
                t = b * IT + it
                dve.wait_ge(e_ready, t + 1)
                dve.tensor_tensor(sm[:, 4:7], E[:], cnt[:, bass.ds(t, 1), :].rearrange("p o k -> p (o k)"), ALU.mult)
                dve.drain()
                dve.tensor_reduce(sm[:, 2:3], sm[:, 4:7], AX_X, ALU.add)
                dve.drain()
                dve.reciprocal(sm[:, 3:4], sm[:, 2:3])
                dve.drain()
                dve.tensor_scalar(pr[:], E[:, 0:2], sm[:, 3:4], None, ALU.mult).then_inc(p_ready, 1)

            def d3(b, it, below):
                t = b * IT + it
                dve.wait_ge(t_ready, t + 1)
                if below:
                    dve.scalar_tensor_tensor(T1[:], PS[:, TAIL_U, G3:2 * G3], pr[:, 1:2], T1[:], ALU.mult, ALU.add)
                    dve.drain()
                dve.tensor_tensor(T1[:, 0:2 * D], T1[:, 0:2 * D], PS[:, TAIL_G, 6 * D:8 * D], ALU.add)
                dve.tensor_tensor(T1[:, 2 * D:G3], T1[:, 2 * D:G3], b_in_sb[:], ALU.add).then_inc(g_ready, 1)

            def d4(b, it):
                t = b * IT + it
                dve.wait_ge(r_ready, t + 1)
                hn = PS[:, TAIL_G, :].rearrange("p (k c) -> p k c", c=D)[:, 0:6:5, :]
                dve.scalar_tensor_tensor(RH[:], TH[:, :, 0:D], 1.0, hn, ALU.add, ALU.mult)
                dve.drain()
                dve.scalar_tensor_tensor(PN[:, 1, :], RH[:, 1, :], 0.5, T1[:, 2 * D:G3], ALU.mult, ALU.add)
                dve.scalar_tensor_tensor(PN[:, 0, :], RH[:, 0, :], 0.5, PS[:, TAIL_G, 3 * D:4 * D], ALU.mult, ALU.add)\
                    .then_inc(pn_ready, 1)

            def d5(b, it):
                t = b * IT + it
                dve.wait_ge(n_ready, t + 1)
                h = H3[:, bass.ds(t, 1), :].to_broadcast([P, 2, D])
                xt = X[:, bass.ds(t, 1), :].rearrange("p o d -> p (o d)")
                dve.tensor_tensor(OO[:], h, NN[:], ALU.subtract)
                dve.drain()
                dve.scalar_tensor_tensor(OO[:], TH[:, :, D:2 * D], 1.0, OO[:], ALU.add, ALU.mult)
                dve.drain()
                dve.scalar_tensor_tensor(OO[:], OO[:], 0.5, NN[:], ALU.mult, ALU.add)
                dve.drain()
                dve.tensor_tensor(RH[:, 0, :], OO[:, 0, :], OO[:, 1, :], ALU.add)
                dve.drain()
                dve.scalar_tensor_tensor(xt, RH[:, 0, :], dN[:, bass.ds(t, 1)], xt, ALU.mult, ALU.add).then_inc(out_ready, 1)

            def pass_block(p, below=False):
                def body(b, first, last):
                    for s in range(NS):
                        if p < 2:
                            out_odd(p, b, s)
                        if p == 0 and first and (g := s // SQ + 1) < RT // LG:
                            if s % SQ == 0:
                                first_norm(g)
                            if s % SQ == 2:
                                second_norm(g)
                        if p == 0:
                            count_above(b, s)
                            if s == NS - 1:
                                take_counts(b)
                        if p < 2 and not first and s == 3:
                            (tail1_a, tail2_a)[p](b - 1)
                        if p < 2 and not first and s == 6:
                            (tail1_b, tail2_b)[p](b - 1)
                        if p == 2:
                            if s == 0 and not first:
                                save3(b - 1, below)
                            mask(b, s, below)
                            if not first:
                                t, k = divmod(s - 2, 3)
                                if 0 <= t < IT:
                                    if k == 0:
                                        d1(b - 1, t)
                                    if k == 1:
                                        d2(b - 1, t)
                                        d3(b - 1, t, below)
                                    if k == 2:
                                        d4(b - 1, t)
                                        d5(b - 1, t)
                            if s == NS - 3:
                                make_diag(b)
                            if s == NS - 1:
                                own_terms(b, below)
                return body

            def first_norm(g):
                t = slice(g * LG, (g + 1) * LG)
                dve.wait_ge(x_loaded[g], 16)
                norm_a(X[:, t, :], LG)
                norm_b(H01[:, t, 0:D], LG, 2 * g)
                dve.drain()
                dve.scalar_tensor_tensor(X[:, t, :], H01[:, t, 0:D], -B_CONST, X[:, t, :], ALU.mult, ALU.add)

            def second_norm(g):
                t = slice(g * LG, (g + 1) * LG)
                dve.drain()
                norm_a(X[:, t, :], LG)
                norm_b(H01[:, t, D:2 * D], LG, 2 * g + 1).then_inc(h_ready, 1)

            def take_products():
                dve.wait_ge(w_loaded, 16 * N_LOADS)
                dve.wait_ge(prod_made, 1)
                for w, k in ((we1_sb, 0), (we2_sb, 1)):
                    dve.tensor_copy(w[:, G3:G3 + 1], PS[:, TAIL_U, k:k + 1])
                    dve.tensor_copy(w[:, G3 + 1:EV], PS[:, TAIL_U, 1 - k:2 - k])
                dve.tensor_copy(v2_sb[:], PS[:, TAIL_U, 2:2 + G3])

            def count_rows():
                dve.memset(own, 0.0)
                dve.drain()
                dve.tensor_scalar(dsign[:, 0, :], dN[:], 0.0, None, ALU.is_gt)
                dve.tensor_scalar(dsign[:, 1, :], dN[:], 0.0, None, ALU.is_lt)
                dve.tensor_tensor(sgn_n[:], pos_n[:], sgn_n[:], ALU.subtract)
                dve.drain()
                dve.tensor_reduce(below_p[:], sgn_n[:], AX_X, ALU.add).then_inc(below_counted, 1)
                dve.tensor_tensor(cnt[:, :, 0], pos_n[:], dsign[:, 0, :], ALU.subtract)
                dve.tensor_tensor(cnt[:, :, 1], sgn_n[:], dsign[:, 1, :], ALU.subtract)
                dve.drain()
                dve.tensor_tensor(sgn_n[:], cnt[:, :, 0], cnt[:, :, 1], ALU.add)
                dve.tensor_scalar(pen[:], cnt[:, :, 0:2], 0.0, ABSENT, ALU.is_equal, ALU.mult)
                dve.drain()
                dve.tensor_scalar(cnt[:, :, 2], sgn_n[:], -1.0, float(N), ALU.mult, ALU.add)
                dve.wait_ge(below_summed, 1)
                dve.tensor_scalar(any_below[:], PS[0:1, TAIL_U, 0:1], 0.0, None, ALU.not_equal).then_inc(any_below_ready, 1)

            dve.memset(eps_sb[:], EPS)
            dve.memset(ones[:], 1.0)
            dve.memset(hT[:], 1.0)
            dve.memset(V[:], NEG_INF).then_inc(consts_made, 1)
            first_norm(0)
            second_norm(0)
            over_blocks(dve, pass_block(0), False)
            tail1_a(NB - 1)
            tail1_b(NB - 1)
            take_products()
            count_rows()
            over_blocks(dve, pass_block(1), False)
            tail2_a(NB - 1)
            tail2_b(NB - 1)

            def pass3(below):
                over_blocks(dve, pass_block(2, below), True)
                save3(NB - 1, below)
                for t in range(IT):
                    d1(NB - 1, t)
                    d2(NB - 1, t)
                    d3(NB - 1, t, below)
                    d4(NB - 1, t)
                    d5(NB - 1, t)

            either_way(dve, pass3)


def kernel(**inputs):
    import concourse.bacc as bacc
    from concourse.bass_utils import run_bass_kernel_spmd

    a = {k: np.asarray(v) for k, v in inputs.items()}
    D = a["x"].shape[1]
    f32 = np.float32

    bd1 = np.zeros((2 * D, 2 * D), f32)
    bd1[:D, :D] = np.eye(D, dtype=f32)
    bd1[D:, D:] = a["L1_gnn_weight"]
    twice = lambda w: np.concatenate([w, w], axis=0)
    wih_e = a["L3_gnn_w_ih_e"]
    haug = np.zeros((D + 2, 8 * D), f32)
    for base, k, cols in ((0, "e", "rzn"), (5 * D, "n", "rz")):
        whh, bih, bhh = a[f"L3_gnn_w_hh_{k}"], a[f"L3_gnn_b_ih_{k}"], a[f"L3_gnn_b_hh_{k}"]
        haug[:D, base:base + D] = whh[2 * D:].T
        haug[D + 1, base:base + D] = bhh[2 * D:]
        haug[:D, base + D:base + 3 * D] = whh[:2 * D].T
        haug[D, base + D:base + 3 * D] = bih[:2 * D]
        haug[D + 1, base + D:base + 3 * D] = bhh[:2 * D]
        if "n" in cols:
            haug[D, base + 3 * D:base + 4 * D] = bih[2 * D:]
    arrays = {
        "x": a["x"], "adj": a["adj"], "bd1": bd1, "w2s": twice(a["L2_gnn_W"]),
        "b2": a["L2_gnn_b"].reshape(1, D),
        "wgat_t2": np.concatenate([a["L3_gnn_W_gat"].T, a["L3_gnn_W_gat"].T], axis=1),
        "a2": np.concatenate([a["L3_gnn_a_gat"][:D], a["L3_gnn_a_gat"][D:]], axis=1),
        "wih_n_t": a["L3_gnn_w_ih_n"].T,
        "b_in": a["L3_gnn_b_ih_n"][2 * D:].reshape(1, D),
        "we1": twice(wih_e[:, :D].T), "we2": twice(wih_e[:, D:].T), "haug": haug,
    }
    nc = bacc.Bacc("TRN2", target_bir_lowering=False, num_devices=1)
    args, maps = [], {}
    for name, v in arrays.items():
        v = np.ascontiguousarray(v)
        maps[f"in_{name}"] = v
        args.append(nc.dram_tensor(f"in_{name}", v.shape, mybir.dt.from_np(v.dtype), kind="ExternalInput").ap())
    out = nc.dram_tensor("out", a["x"].shape, F32, kind="ExternalOutput").ap()
    gnn_stack(nc, *args, out)
    r = run_bass_kernel_spmd(nc, [maps], core_ids=[0])
    return r.results[0]["out"]
```

```python
from contextlib import ExitStack

import numpy as np

import concourse.bass as bass
from concourse import mybir

F32 = mybir.dt.float32
F32R = mybir.dt.float32r
BF16 = mybir.dt.bfloat16
ALU = mybir.AluOpType
ACT = mybir.ActivationFunctionType
AX_X = mybir.AxisListType.X

P = 128
EPS = 1e-5
F_CONST, B_CONST, R_CONST = 1.0, 0.1, 0.01
ALPHA = 0.2
NEG_INF = -9000000000000000.0
ABSENT = -3.0e38


def gnn_stack(nc, x, adj, bd1, w2s, b2, wgat_t2, a2, wih_n_t, b_in, we1, we2, haug, out):
    N, D = x.shape
    RT = N // P
    IT = 4
    BLK = IT * P
    NB = N // BLK
    NQ = 4
    QC = N // NQ
    NT = N // P
    NS = NT // 2
    SQ = NS // NQ
    G3 = 3 * D
    EV = G3 + 2
    NODE = 4 * D + 2
    GATES = NODE + G3

    GT = 4
    NG = NT // GT
    NSLOT = 4

    turned_dram = nc.dram_tensor("turned_adj", (NB, NG, P, GT * BLK), F32, kind="Internal").ap()
    turned_chunks = turned_dram.rearrange("b (q g) p n -> b q p g n", q=NQ)
    diag_dram = nc.dram_tensor("diagonal", (N,), F32, kind="Internal").ap()
    turned_back = bass.AP(tensor=turned_dram.tensor, offset=turned_chunks[NB - 1].offset,
                          ap=[[-NT * P * BLK, NB]] + [list(d) for d in turned_chunks[0].ap])
    adj_blocks = adj.rearrange("(b t p) j -> b p t j", t=IT, p=P)
    x_rows = x.rearrange("(t p) d -> p t d", p=P)
    out_rows = out.rearrange("(b t p) d -> b p t d", t=IT, p=P)

    with ExitStack() as ctx:
        def sb(name, shape, dt=F32):
            return ctx.enter_context(nc.sbuf_tensor(name, shape, dt))

        def sem(name):
            return ctx.enter_context(nc.semaphore(name))

        PS = ctx.enter_context(nc.psum_tensor("PS", [P, 8, 512], F32))
        TURN, ACC_A, ACC_P, ACC_M, ACC_N, TAIL, TAIL2 = 0, 2, 3, 4, 5, 6, 7
        G4 = PS[:, 4:8, :]
        U4 = PS[:, 0:2, 0:2 * G3].rearrange("p b (h g) -> p b h g", h=2)
        G1, U1 = PS[:, 6:7, :], PS[:, 0, :]

        nat = sb("nat", [P, NQ, IT, QC])
        chunk = nat[:].rearrange("p q t (k n) -> p q (t k) n", n=BLK)
        spill = sb("spill", [P, NSLOT * GT * BLK])
        groups = spill[:].rearrange("p (g k n) -> p g k n", g=NSLOT, k=GT)
        H3T = spill[0:D, 0:N]
        low = spill[:, N:N + 4 * BLK].rearrange("p (k n) -> p k n", k=4)
        own = spill[:, N + 4 * BLK:N + 8 * BLK].rearrange("p (k n) -> p k n", k=4)
        pos = sb("pos", [P, 8, BLK], F32R)
        neg = sb("neg", [P, 4, BLK], F32R)
        X = sb("X", [P, RT, D])
        H_buf = sb("H_buf", [P, RT * 2 * D])
        H01 = H_buf[:].rearrange("p (t d) -> p t d", t=RT)
        H3 = H_buf[:, 0:RT * D].rearrange("p (t d) -> p t d", t=RT)
        RH, PN, NN, OO = (H_buf[:, RT * D + k * 2 * IT * D:RT * D + (k + 1) * 2 * IT * D]
                          .rearrange("p (k t d) -> p k t d", k=2, t=IT) for k in range(4))
        H2 = sb("H2", [P, RT, D])
        H3HL = sb("H3HL", [P, RT, 2 * D], F32R)
        hT = sb("hT", [D + 2, BLK])
        saved = sb("saved", [P, 4, BLK])
        diag_rows = sb("diag_rows", [RT, P])
        wide_d = sb("wide_d", [D, BLK])
        ident = sb("ident", [P, P])
        ones = sb("ones", [P, 1])
        dN = sb("dN", [P, RT])
        b2_sb = sb("b2_sb", [P, D])
        b_in_sb = sb("b_in_sb", [P, D])
        bd1_sb = sb("bd1_sb", [P, 2 * D])
        w2s_sb = sb("w2s_sb", [P, D])
        wg_sb = sb("wg_sb", [D, 2 * D])
        a2_sb = sb("a2_sb", [D, 2])
        wn_sb = sb("wn_sb", [D, G3])
        we1_sb = sb("we1_sb", [P, EV])
        we2_sb = sb("we2_sb", [P, EV])
        haug_sb = sb("haug_sb", [D + 2, GATES])
        v2_sb = sb("v2_sb", [P, G3])
        eps_sb = sb("eps_sb", [P, 1])
        LG = 8
        xc = sb("xc", [P, LG, D])
        sq = sb("sq", [P, LG, D])
        st = sb("st", [P, 5, LG])
        hrow = sb("hrow", [P, IT, D])
        wrow = sb("wrow", [P, IT, D])
        sgn_blk = sb("sgn_blk", [P, IT, NQ])
        pos_blk = sb("pos_blk", [P, IT, NQ])
        sgn_n = sb("sgn_n", [P, RT])
        pos_n = sb("pos_n", [P, RT])
        junk_a = sb("junk_a", [P, QC], BF16)
        junk_v = sb("junk_v", [P, QC], BF16)
        dsign = sb("dsign", [P, 2, RT])
        cnt = sb("cnt", [P, RT, 3])
        pen = sb("pen", [P, RT, 2])
        below_p = sb("below_p", [P, 1])
        any_below = sb("any_below", [1, 1], mybir.dt.int32)
        V = sb("V", [P, IT, 3])
        E = sb("E", [P, IT, 3])
        sm = sb("sm", [P, 4, IT])
        row_term = sb("row_term", [P, 2, IT])
        pr = sb("pr", [P, IT, 2])
        T1 = sb("T1", [P, IT, G3])
        TH = sb("TH", [P, 2, IT, 2 * D])

        x_loaded = [sem(f"x_loaded{i}") for i in range(RT // LG)]
        bd1_loaded = sem("bd1_loaded")
        w_loaded = sem("w_loaded")
        nat_loaded = [sem(f"nat_loaded{i}") for i in range(NQ)]
        ident_made = sem("ident_made")
        consts_made = sem("consts_made")
        prod_made = sem("prod_made")
        prod_saved = sem("prod_saved")
        turned = sem("turned")
        spilled = [sem(f"spilled{i}") for i in range(NSLOT)]
        step_used = sem("step_used")
        even_out = sem("even_out")
        odd_out = sem("odd_out")
        signs_done = sem("signs_done")
        above_done = sem("above_done")
        counts_taken = sem("counts_taken")
        masked = sem("masked")
        acc_full = sem("acc_full")
        acc_saved = sem("acc_saved")
        sums_a = sem("sums_a")
        var_ready = sem("var_ready")
        std_ready = sem("std_ready")
        h_ready = sem("h_ready")
        tail_ready = sem("tail_ready")
        rows_ready = sem("rows_ready")
        hT_made = sem("hT_made")
        hT_saved = sem("hT_saved")
        hT_block = sem("hT_block")
        diag_turned = sem("diag_turned")
        diag_stored = sem("diag_stored")
        wide_loaded = sem("wide_loaded")
        own_made = sem("own_made")
        value_gates = sem("value_gates")
        v_ready = sem("v_ready")
        e_ready = sem("e_ready")
        p_ready = sem("p_ready")
        t_ready = sem("t_ready")
        g_ready = sem("g_ready")
        r_ready = sem("r_ready")
        pn_ready = sem("pn_ready")
        n_ready = sem("n_ready")
        out_ready = sem("out_ready")
        stored = sem("stored")
        below_counted = sem("below_counted")
        any_below_ready = sem("any_below_ready")

        block = ctx.enter_context(nc.Block())

        def over_blocks(eng, body, last_apart, after_first=None):
            body(0, True, False)
            if after_first:
                after_first()
            with eng.Fori(1, NB - 1 if last_apart else NB) as b:
                body(b, False, False)
            if last_apart:
                body(NB - 1, False, True)

        def either_way(eng, pass3):
            eng.wait_ge(any_below_ready, 1)
            some = eng.value_load(any_below[0:1, 0:1], min_val=0, max_val=1)
            with eng.If(some != 0):
                pass3(True)
            with eng.Else():
                pass3(False)

        def sums_saved(b, below):
            return 2 * NB + b * (4 if below else 2)

        def group_free(eng, b, g):
            if not (isinstance(b, int) and b == 0 and g < NSLOT):
                eng.wait_ge(spilled[g % NSLOT], 16 * (b * (NG // NSLOT) + g // NSLOT))

        def all_spilled(eng):
            for k in range(NSLOT):
                eng.wait_ge(spilled[k], 16 * (NG // NSLOT) * NB)

        def block_of(p, i):
            return i if p != 1 else NB - 1 - i

        def step_of(p, s):
            return s if p == 0 else (s + NS // 2) % NS

        def loads_done(p, i, q):
            return 16 * (p * NB + i + 1 - (0 if p == 0 else p - 1 + (q >= NQ // 2)))

        @block.sync
        def _(sp):
            def load_x(g):
                sp.dma_start(X[:, g * LG:(g + 1) * LG, :], x_rows[:, g * LG:(g + 1) * LG, :]).then_inc(x_loaded[g], 16)

            def load_adj(b, q):
                sp.dma_start(nat[:, q, :, :], adj_blocks[b, :, :, q * QC:(q + 1) * QC]).then_inc(nat_loaded[q], 16)

            def spill_group(b, g):
                sp.wait_ge(even_out, b * NS + (g + 1) * GT // 2)
                sp.wait_ge(odd_out, b * NS + (g + 1) * GT // 2)
                sp.dma_start(turned_dram[b, g], spill[:, (g % NSLOT) * GT * BLK:(g % NSLOT + 1) * GT * BLK])\
                  .then_inc(spilled[g % NSLOT], 16)

            def load_turned(chunks, b, q):
                sp.dma_start(chunk[:, q, :, :].rearrange("p (g k) n -> p g (k n)", k=GT),
                             chunks[b, q]).then_inc(nat_loaded[q], 16)

            load_x(0)
            load_adj(0, 0)
            sp.dma_start(bd1_sb[:], bd1).then_inc(bd1_loaded, 16)
            for g in range(1, RT // LG):
                load_x(g)
            for q in range(1, NQ):
                load_adj(0, q)
            for q in range(NQ):
                spill_group(0, 2 * q)
                spill_group(0, 2 * q + 1)
                sp.wait_ge(turned, (q + 1) * 2 * SQ + 4)
                sp.wait_ge(above_done, (q + 1) * SQ)
                load_adj(1, q)
            with sp.Fori(2, NB) as b:
                for q in range(NQ):
                    spill_group(b - 1, 2 * q)
                    spill_group(b - 1, 2 * q + 1)
                    sp.wait_ge(turned, (b - 1) * NT + (q + 1) * 2 * SQ + 4)
                    load_adj(b, q)
            spill_group(NB - 1, 0)
            for q in range(NQ):
                for g in range(2 * q + 1, min(2 * q + 3, NG)):
                    spill_group(NB - 1, g)
                if q < NQ // 2:
                    for g in (2 * q, 2 * q + 1):
                        sp.wait_ge(spilled[g], 16 * ((NG // NSLOT) * NB - 1))
                sp.wait_ge(turned, min((NB - 1) * NT + (q + 1) * 2 * SQ + 4, NB * NT))
                if q == NQ - 1:
                    sp.wait_ge(signs_done, NB * NQ * IT)
                    sp.wait_ge(above_done, NB * NQ * IT)
                load_turned(turned_back, 0 if q < NQ // 2 else 1, q)
            for q in range(NQ // 2):
                sp.wait_ge(step_used, NS // 2 + (q + 1) * SQ)
                load_turned(turned_back, 1, q)
            with sp.Fori(2, NB) as i:
                for k in range(NQ):
                    sp.wait_ge(step_used, (i - 1) * NS + (k + 1) * SQ)
                    load_turned(turned_back, i, (k + NQ // 2) % NQ)
            all_spilled(sp)
            with sp.Fori(0, NB - 1) as b:
                for k in range(NQ):
                    sp.wait_ge(step_used, (NB + b) * NS + (k + 1) * SQ)
                    load_turned(turned_chunks[1:], b, (k + NQ // 2) % NQ)

        @block.gpsimd
        def _(pool):
            nc.gpsimd.memset(ident[:], 0.0)
            pool.drain()
            nc.gpsimd.affine_select(out=ident[:], in_=ident[:], compare_op=ALU.not_equal, fill=1.0, base=0,
                                    pattern=[[-1, P]], channel_multiplier=1).then_inc(ident_made, 1)
            with nc.allow_non_contiguous_dma(reason="the diagonal"):
                loads = [(w2s_sb, w2s), (wg_sb, wgat_t2), (a2_sb, a2), (wn_sb, wih_n_t),
                         (we1_sb, we1), (we2_sb, we2), (haug_sb, haug),
                         (b2_sb, b2.to_broadcast([P, D])), (b_in_sb, b_in.to_broadcast([P, D]))]
                for dst, src in loads:
                    pool.dma_start(dst[:, 0:src.shape[1]], src).then_inc(w_loaded, 16)
                diag = bass.AP(tensor=adj.tensor, offset=adj.offset, ap=[[N + 1, P], [P * (N + 1), RT], [1, 1]])
                pool.dma_start(dN[:].rearrange("p (t o) -> p t o", o=1), diag).then_inc(w_loaded, 16)
            pool.wait_ge(diag_turned, 1)
            pool.dma_start(diag_dram.rearrange("(t p) -> t p", p=P), diag_rows[:]).then_inc(diag_stored, 16)
            pool.wait_ge(diag_stored, 16)

            def load_wide(b):
                src = diag_dram.rearrange("(b o n) -> b o n", b=NB, o=1)[b]
                pool.dma_start(wide_d[:], src.to_broadcast([D, BLK])).then_inc(wide_loaded, 16)

            def store(b):
                pool.wait_ge(out_ready, b * IT + IT)
                pool.dma_start(out_rows[b], X[:, bass.ds(b * IT, IT), :]).then_inc(stored, 16)

            load_wide(0)
            pool.wait_ge(own_made, 1)
            load_wide(1)
            with pool.Fori(0, NB - 2) as b:
                pool.wait_ge(own_made, b + 2)
                load_wide(b + 2)
                store(b)
            store(NB - 2)
            store(NB - 1)
            pool.wait_ge(stored, 16 * NB)

        N_LOADS = 10
        BOTH = 3 * SQ
        TAIL_STEPS = (3, 4, 5, 6, 7, 9)

        @block.tensor
        def _(pe):
            def turn(b, s):
                if s % SQ == 0:
                    pe.wait_ge(nat_loaded[(s // SQ) % NQ], 16 * (b + s // NS + 1))
                for c in (2 * s, 2 * s + 1):
                    q, k = (c // (2 * SQ)) % NQ, c % (2 * SQ)
                    for it in range(IT):
                        ins = pe.transpose(PS[:, TURN + c % 2, it * P:(it + 1) * P],
                                           nat[:, q, it, k * P:(k + 1) * P], ident[:])
                    ins.then_inc(turned, 1)

            def products(p, b, s, below, first):
                cs = (2 * step_of(p, s), 2 * step_of(p, s) + 1)
                for c in cs:
                    if p == 0 or (p == 1 and first and s < NS // 2):
                        A = groups[:, (c // GT) % NSLOT, c % GT, :]
                    else:
                        A = chunk[:, c // (2 * SQ), c % (2 * SQ), :]
                    if p == 0:
                        ins = pe.matmul(PS[:, ACC_A, :], H01[:, c, :], A, start=c == 0, stop=c == NT - 1)
                    else:
                        half = slice(D * (c % 2), D * (c % 2) + D)
                        ins = pe.matmul(PS[half, ACC_A, :], (H2, H3)[p - 1][:, c, :], A, start=s == 0, stop=s == NS - 1)
                if p == 2:
                    if s == NS - 1:
                        ins.then_inc(sums_a, 1)
                    for j, c in enumerate(cs):
                        half = slice(D * (c % 2), D * (c % 2) + D)
                        pe.matmul(PS[half, ACC_N, :], H3[:, c, :], low[:, (2 * s + j) % 4, :], start=s == 0, stop=s == NS - 1)
                    if s == 0 and not first:
                        pe.wait_ge(acc_saved, sums_saved(b, below))
                    at = dict(start=s == 0, stop=False), dict(start=False, stop=s == NS - 1)
                    for j, c in enumerate(cs):
                        pe.matmul(PS[:, ACC_P, :], H3HL[:, c, :], pos[:, (2 * s + j) % 8, :], **at[j])
                    for j, c in enumerate(cs):
                        ins = pe.matmul(PS[:, ACC_M, :], H3HL[:, c, :], neg[:, (2 * s + j) % 4, :], **at[j])
                if p > 0:
                    ins.then_inc(step_used, 1)
                elif s == NS - 1:
                    ins.then_inc(acc_full, 1)

            def products_above(b, s, first):
                tiles = [2 * step_of(2, s - s % 2) + j for j in range(4)]
                if s % 2 == 0:
                    for j, c in enumerate(tiles):
                        half = slice(D * (c % 2), D * (c % 2) + D)
                        ins = pe.matmul(PS[half, ACC_A, :], H3[:, c, :], chunk[:, c // (2 * SQ), c % (2 * SQ), :],
                                        start=s == 0 and j < 2, stop=s == NS - 2 and j >= 2)
                    if s == NS - 2:
                        ins.then_inc(sums_a, 1)
                else:
                    if s == 1 and not first:
                        pe.wait_ge(acc_saved, sums_saved(b, False))
                    for j, c in enumerate(tiles):
                        ins = pe.matmul(PS[:, ACC_P, :], H3HL[:, c, :], pos[:, (2 * s - 2 + j) % 8, :],
                                        start=s == 1 and j == 0, stop=s == NS - 1 and j == 3)
                        if j % 2 == 1:
                            ins.then_inc(step_used, 1)

            def tail12(p, b):
                pe.wait_ge(acc_saved, p * NB + b + 1)
                for it in range(IT):
                    rows = saved[:, 0, it * P:(it + 1) * P]
                    w, n = ((bd1_sb, 2 * D), (w2s_sb, D))[p]
                    ins = pe.matmul(PS[:, TAIL, it * n:(it + 1) * n], rows, w[:], start=True, stop=True)
                ins.then_inc(tail_ready, 1)

            def turn_h3(b):
                for it in range(IT):
                    ins = pe.transpose(PS[0:D, TAIL2, it * P:(it + 1) * P], hrow[:, it, :], ident[:])
                ins.then_inc(hT_made, 1)

            def hidden_gates(b, it):
                if it == 0:
                    pe.wait_ge(hT_block, b + 1)
                    if not (isinstance(b, int) and b == 0):
                        pe.wait_ge(pn_ready, b)
                pe.matmul(G4[:, it, 0:GATES], hT[:, it * P:(it + 1) * P], haug_sb[:], start=True, stop=False, skip_group_check=True)

            def gates_above(b):
                for it in range(IT):
                    ins = pe.matmul(G4[:, it, D:D + EV], saved[:, 1, it * P:(it + 1) * P], we1_sb[:],
                                    start=False, stop=True, skip_group_check=True)
                ins.then_inc(tail_ready, 1)

            def attended_gates(b):
                for it in range(IT):
                    ins = pe.matmul(U4[:, it // 2, it % 2, :], saved[:, 0, it * P:(it + 1) * P], v2_sb[:], start=True, stop=True)
                ins.then_inc(value_gates, 1)

            def tail3(b, it):
                cols = slice(it * P, (it + 1) * P)
                if it == 0:
                    pe.wait_ge(acc_saved, sums_saved(b + 1, True))
                    pe.wait_ge(hT_block, b + 1)
                else:
                    pe.wait_ge(pn_ready, b * IT + it)
                G = G1[:, 0, :]
                pe.matmul(G[:, 0:GATES], hT[:, cols], haug_sb[:], start=True, stop=False, skip_group_check=True)
                pe.matmul(G[:, D:D + EV], saved[:, 1, cols], we1_sb[:], start=False, stop=False, skip_group_check=True)
                pe.matmul(G[:, D:D + EV], saved[:, 2, cols], we2_sb[:], start=False, stop=True, skip_group_check=True)
                pe.matmul(U1[:, G3:2 * G3], saved[:, 3, cols], v2_sb[:], start=True, stop=True)
                pe.matmul(U1[:, 0:G3], saved[:, 0, cols], v2_sb[:], start=True, stop=True).then_inc(tail_ready, 1)

            def pass_block(p, below=False):
                def body(b, first, last):
                    for s in range(NS):
                        if p == 0:
                            pe.wait_ge(even_out, b * NS + s + 1)
                            pe.wait_ge(odd_out, b * NS + s + 1)
                            if not (last and s == NS - 1):
                                turn(b, s + 1)
                        elif s % SQ == 0 and not (p == 1 and first and s < NS // 2):
                            q = step_of(p, s) // SQ
                            pe.wait_ge(nat_loaded[q], loads_done(p, b, q))
                        if s == 0 and not first:
                            pe.wait_ge(acc_saved, p * NB + b if p < 2 else sums_saved(b - 1, below) + (2 if below else 1))
                        if first and p == 0 and (2 * s) % LG == 0:
                            pe.wait_ge(h_ready, 2 * s // LG + 1)
                        if first and p == 1 and s == 0:
                            pe.wait_ge(rows_ready, NB - 1)
                        if first and p == 1 and s == NS // 2 - 2:
                            pe.wait_ge(rows_ready, NB)
                        if p == 2 and (below or s % 2 == 1):
                            pe.wait_ge(masked, b * NS + s + 1)
                        if not first and p == 1 and s == 9:
                            pe.wait_ge(rows_ready, NB + b)
                        if p == 2 and not below:
                            products_above(b, s, first)
                        else:
                            products(p, b, s, below, first)
                        if not first and p < 2 and s == 2:
                            tail12(p, b - 1)
                        if not first and p == 1 and s == 9:
                            turn_h3(b - 1)
                        if not first and p == 2 and below and s in (1, 4, 7, 10):
                            tail3(b - 1, (s - 1) // 3)
                        if not first and p == 2 and not below and s == 1:
                            gates_above(b - 1)
                        if not first and p == 2 and not below and s == 3:
                            attended_gates(b - 1)
                        if first and p == 2 and not below and s == 5:
                            pe.wait_ge(rows_ready, 2 * NB)
                            turn_h3(NB - 1)
                        if p == 2 and not below and s >= NS - IT:
                            hidden_gates(b, s - (NS - IT))
                return body

            pe.wait_ge(ident_made, 1)
            pe.wait_ge(consts_made, 1)
            turn(0, 0)
            pe.wait_ge(bd1_loaded, 16)
            over_blocks(pe, pass_block(0), True)
            tail12(0, NB - 1)

            def weight_products():
                pe.wait_ge(w_loaded, 16 * N_LOADS)
                pe.matmul(PS[:, TAIL2, 0:2], wg_sb[:], a2_sb[:], start=True, stop=True)
                pe.transpose(PS[0:RT, TAIL2, 256:256 + P], dN[:], ident[:])
                pe.matmul(PS[:, TAIL2, 2:2 + G3], wg_sb[:], wn_sb[:], start=True, stop=True)
                pe.wait_ge(below_counted, 1)
                pe.matmul(PS[0:1, TAIL2, 508:509], below_p[:], ones[:], start=True, stop=True).then_inc(prod_made, 1)

            over_blocks(pe, pass_block(1), False, after_first=weight_products)
            tail12(1, NB - 1)

            def pass3(below):
                if below:
                    pe.wait_ge(rows_ready, 2 * NB)
                    turn_h3(NB - 1)
                else:
                    pe.wait_ge(rows_ready, 2 * NB - 1)
                over_blocks(pe, pass_block(2, below), False)
                if below:
                    for it in range(IT):
                        tail3(NB - 1, it)
                else:
                    pe.wait_ge(acc_saved, sums_saved(NB, False))
                    gates_above(NB - 1)
                    attended_gates(NB - 1)

            either_way(pe, pass3)

        @block.scalar
        def _(act):
            def out_even(b, s):
                g, k = divmod(2 * s, GT)
                act.wait_ge(turned, b * NT + 2 * s + 1)
                if k == 0:
                    group_free(act, b, g)
                nc.scalar.copy(groups[:, g % NSLOT, k, :], PS[:, TURN, :]).then_inc(even_out, 1)

            def out_odd_too(s):
                g, k = divmod(2 * s + 1, GT)
                act.wait_ge(turned, 2 * s + 2)
                nc.scalar.copy(groups[:, g % NSLOT, k, :], PS[:, TURN + 1, :]).then_inc(odd_out, 1)

            def count_signs(b, s, first):
                q, it = s // SQ, s % SQ
                act.drain()
                if s == 0 and not first:
                    act.wait_ge(counts_taken, b)
                nc.scalar.activation(junk_a[:], nat[:, q, it, :], ACT.Sign,
                                     accum_out=sgn_blk[:, it, q:q + 1]).then_inc(signs_done, 1)

            def save(p, b):
                act.wait_ge(*((acc_full, b + 1) if p == 0 else (step_used, (b + 1) * NS)))
                nc.scalar.copy(saved[:, 0, :], PS[:, ACC_A, :]).then_inc(acc_saved, 1)

            def deviations(n_before, tiles):
                act.wait_ge(var_ready, n_before + 1)
                nc.scalar.activation(st[:, 3, 0:tiles], st[:, 2, 0:tiles], ACT.Sqrt, bias=eps_sb[:],
                                     scale=1.0 / D).then_inc(std_ready, 1)

            def save_h3t(b):
                act.wait_ge(hT_made, b + 1)
                nc.scalar.copy(H3T[:, bass.ds(block_of(1, b) * BLK, BLK)], PS[0:D, TAIL2, :]).then_inc(hT_saved, 1)

            def fetch_hT(b):
                nc.scalar.copy(hT[0:D, :], H3T[:, bass.ds(b * BLK, BLK)]).then_inc(hT_block, 1)

            def a1(u, G, n):
                act.wait_ge(v_ready, u + 1)
                nc.scalar.activation(E[:, 0:n, :], V[:, 0:n, :], ACT.Exp)
                nc.scalar.activation(TH[:, 0, 0:n, :], G[:, :, D:3 * D], ACT.Tanh, scale=0.5).then_inc(e_ready, 1)

            def a2_(u, U, n):
                if n == IT:
                    act.wait_ge(value_gates, u + 1)
                act.wait_ge(p_ready, u + 1)
                for k in range(n):
                    src = U[:, 0:G3] if n == 1 else U[:, k // 2, k % 2, :]
                    ins = nc.scalar.activation(T1[:, k, :], src, ACT.Copy, scale=pr[:, k, 0:1])
                ins.then_inc(t_ready, 1)

            def a3(u, n):
                act.wait_ge(g_ready, u + 1)
                nc.scalar.activation(TH[:, 1, 0:n, :], T1[:, 0:n, 0:2 * D], ACT.Tanh, scale=0.5).then_inc(r_ready, 1)

            def a4(u, n):
                act.wait_ge(pn_ready, u + 1)
                nc.scalar.activation(NN[:, :, 0:n, :], PN[:, :, 0:n, :], ACT.Tanh).then_inc(n_ready, 1)

            def tail3_step(b, s, below):
                if below:
                    t, k = divmod(s - 2, 3)
                    if not 0 <= t < IT:
                        return
                    u, G, U, n = b * IT + t, G1, U1, 1
                else:
                    if s not in (5, 7, 9):
                        return
                    k, u, G, U, n = (s - 5) // 2, b, G4, U4, IT
                if k == 0:
                    a1(u, G, n)
                if k == 1:
                    a2_(u, U, n)
                    a3(u, n)
                if k == 2:
                    a4(u, n)

            def pass_block(p, below=False):
                def body(b, first, last):
                    for s in range(NS):
                        if p == 0:
                            out_even(b, s)
                            if first and s < BOTH:
                                out_odd_too(s)
                        if not first and s == 0 and p < 2:
                            save(p, b - 1)
                        if p == 0 and first and s // SQ + 1 < RT // LG and s % 2 == 0:
                            deviations(2 * (s // SQ + 1) + s % SQ // 2, LG)
                        if p == 0:
                            count_signs(b, s, first)
                        if not first and p < 2 and s == TAIL_STEPS[-1]:
                            deviations(2 * (RT // LG) + p * NB + b - 1, IT)
                        if not first and p == 1 and s == 10:
                            save_h3t(b - 1)
                        if p == 2:
                            if not first:
                                tail3_step(b - 1, s, below)
                            if s == (NS - 2 if below else 10):
                                fetch_hT(b)
                return body

            act.wait_ge(consts_made, 1)
            nc.scalar.activation(st[:, 3, 0:1], eps_sb[:], ACT.Sqrt)
            act.drain()
            for n in range(2):
                deviations(n, LG)
            over_blocks(act, pass_block(0), True)
            save(0, NB - 1)
            deviations(2 * (RT // LG) + NB - 1, IT)
            all_spilled(act)
            over_blocks(act, pass_block(1), False)
            save(1, NB - 1)
            deviations(2 * (RT // LG) + 2 * NB - 1, IT)
            save_h3t(NB - 1)
            act.drain()

            def pass3(below):
                over_blocks(act, pass_block(2, below), False)
                for s in range(NS):
                    tail3_step(NB - 1, s, below)

            either_way(act, pass3)

        @block.vector
        def _(dve):
            def wide(col, n):
                return col.rearrange("p (t o) -> p t o", o=1).to_broadcast([P, n, D])

            def norm_a(src, tiles):
                dve.tensor_reduce(st[:, 0, 0:tiles], src, AX_X, ALU.add)
                dve.drain()
                dve.tensor_scalar(st[:, 1, 0:tiles], st[:, 0, 0:tiles], 1.0 / D, None, ALU.mult)
                dve.drain()
                dve.tensor_tensor(xc[:, 0:tiles, :], src, wide(st[:, 1, 0:tiles], tiles), ALU.subtract)
                dve.drain()
                dve.tensor_tensor(sq[:, 0:tiles, :], xc[:, 0:tiles, :], xc[:, 0:tiles, :], ALU.mult)
                dve.drain()
                dve.tensor_reduce(st[:, 2, 0:tiles], sq[:, 0:tiles, :], AX_X, ALU.add).then_inc(var_ready, 1)

            def norm_b(dst, tiles, n_before):
                dve.wait_ge(std_ready, n_before + 1)
                dve.reciprocal(st[:, 4, 0:tiles], st[:, 3, 0:tiles])
                dve.drain()
                return dve.scalar_tensor_tensor(dst, xc[:, 0:tiles, :], 0.0, wide(st[:, 4, 0:tiles], tiles),
                                                ALU.max, ALU.mult)

            def out_odd(b, s):
                g, k = divmod(2 * s + 1, GT)
                dve.wait_ge(turned, b * NT + 2 * s + 2)
                if k == 1:
                    group_free(dve, b, g)
                dve.tensor_copy(groups[:, g % NSLOT, k, :], PS[:, TURN + 1, :]).then_inc(odd_out, 1)

            def count_above(b, s):
                q, it = s // SQ, s % SQ
                dve.drain()
                dve.tensor_scalar(junk_v[:], nat[:, q, it, :], 0.0, None, ALU.is_gt, ALU.add,
                                  accum_out=pos_blk[:, it, q:q + 1]).then_inc(above_done, 1)

            def take_counts(b):
                dve.drain()
                dve.wait_ge(signs_done, (b + 1) * NQ * IT)
                dve.tensor_reduce(sgn_n[:, bass.ds(b * IT, IT)], sgn_blk[:], AX_X, ALU.add)
                dve.tensor_reduce(pos_n[:, bass.ds(b * IT, IT)], pos_blk[:], AX_X, ALU.add).then_inc(counts_taken, 1)

            def norm_step(src, tiles, k):
                dve.drain()
                if k == 0:
                    dve.tensor_reduce(st[:, 0, 0:tiles], src, AX_X, ALU.add)
                    dve.drain()
                    dve.tensor_scalar(st[:, 1, 0:tiles], st[:, 0, 0:tiles], 1.0 / D, None, ALU.mult)
                if k == 1:
                    dve.tensor_tensor(xc[:, 0:tiles, :], src, wide(st[:, 1, 0:tiles], tiles), ALU.subtract)
                    dve.drain()
                    dve.tensor_tensor(sq[:, 0:tiles, :], xc[:, 0:tiles, :], xc[:, 0:tiles, :], ALU.mult)
                if k == 2:
                    dve.tensor_reduce(st[:, 2, 0:tiles], sq[:, 0:tiles, :], AX_X, ALU.add).then_inc(var_ready, 1)

            def tail1_step(b, k):
                t = bass.ds(b * IT, IT)
                if k == 0:
                    dve.wait_ge(tail_ready, b + 1)
                    Q = PS[:, TAIL, :].rearrange("p (t n) -> p t n", t=IT)
                    dve.tensor_tensor(wrow[:], Q[:, :, 0:D], H01[:, t, 0:D], ALU.mult)
                    dve.tensor_tensor(X[:, t, :], X[:, t, :], Q[:, :, D:2 * D], ALU.add)
                if k == 1:
                    dve.drain()
                    dve.tensor_reduce(row_term[:, 0, :], wrow[:], AX_X, ALU.add)
                    dve.drain()
                    dve.tensor_scalar(row_term[:, 1, :], row_term[:, 0, :], -R_CONST, F_CONST, ALU.mult, ALU.add)
                    dve.drain()
                    dve.tensor_tensor(X[:, t, :], X[:, t, :], wide(row_term[:, 1, :], IT), ALU.add)
                if k in (2, 3, 4):
                    norm_step(X[:, t, :], IT, k - 2)
                if k == 5:
                    norm_b(H2[:, t, :], IT, 2 * (RT // LG) + b).then_inc(rows_ready, 1)

            def tail2_step(i, k):
                t = bass.ds(block_of(1, i) * IT, IT)
                if k == 0:
                    dve.wait_ge(tail_ready, NB + i + 1)
                    Q = PS[:, TAIL, 0:IT * D].rearrange("p (t n) -> p t n", t=IT)
                    dve.tensor_tensor(X[:, t, :], X[:, t, :], b2_sb[:].rearrange("p (o d) -> p o d", o=1).to_broadcast([P, IT, D]), ALU.add)
                    dve.drain()
                    dve.tensor_tensor(X[:, t, :], X[:, t, :], Q, ALU.add)
                if k in (2, 3, 4):
                    norm_step(X[:, t, :], IT, k - 2)
                if k == 5:
                    norm_b(hrow[:], IT, 2 * (RT // LG) + NB + i)
                    dve.drain()
                    dve.tensor_copy(H3[:, t, :], hrow[:])
                    dve.tensor_copy(H3HL[:, t, 0:D], hrow[:])
                    dve.drain()
                    dve.tensor_tensor(H3HL[:, t, D:2 * D], hrow[:], H3HL[:, t, 0:D].bitcast(F32), ALU.subtract).then_inc(rows_ready, 1)

            def mask(b, s, below):
                b, s = b + s // NS, s % NS
                if s % SQ == 0:
                    dve.wait_ge(nat_loaded[step_of(2, s) // SQ], loads_done(2, b, step_of(2, s) // SQ))
                held = 2 if below else 4
                if not (isinstance(b, int) and b == 0 and s < held):
                    dve.wait_ge(step_used, NB * NS + b * NS + s + 1 - held)
                tiles = [(2 * s + j, chunk[:, c // (2 * SQ), c % (2 * SQ), :])
                         for j, c in enumerate((2 * step_of(2, s), 2 * step_of(2, s) + 1))]
                for k, A in tiles:
                    ins = dve.tensor_scalar(pos[:, k % 8, :], A, 0.0, None, ALU.is_gt)
                for k, A in tiles if below else ():
                    dve.tensor_scalar(neg[:, k % 4, :], A, 0.0, None, ALU.is_lt)
                    dve.tensor_scalar(low[:, k % 4, :], A, 0.0, None, ALU.min)
                if below:
                    dve.drain()
                for k, A in tiles if below else ():
                    ins = dve.tensor_scalar(A, A, 0.0, None, ALU.max)
                ins.then_inc(masked, 1)

            def own_terms(b, below):
                dve.drain()
                dve.wait_ge(wide_loaded, 16 * (b + 1))
                if isinstance(b, int) and b == 0:
                    dve.wait_ge(hT_saved, NB)
                for k, op in ((0, ALU.max), (1, ALU.is_gt), (2, ALU.is_lt), (3, ALU.min))[:4 if below else 2]:
                    ins = dve.scalar_tensor_tensor(own[0:D, k, :], wide_d[:], 0.0, H3T[:, bass.ds(b * BLK, BLK)], op, ALU.mult)
                ins.then_inc(own_made, 1)

            def save3(b, below):
                dve.drain()
                dve.wait_ge(sums_a, b + 1)
                for n, (k, bank) in enumerate(((0, ACC_A), (3, ACC_N), (1, ACC_P), (2, ACC_M)) if below
                                              else ((0, ACC_A), (1, ACC_P))):
                    if n == 1:
                        dve.wait_ge(step_used, (NB + b + 1) * NS)
                    dve.tensor_tensor(saved[:, k, :], PS[:, bank, :], own[:, k, :], ALU.subtract).then_inc(acc_saved, 1)

            def last_dim(ap, n, w):
                return ap.rearrange("p (t o) -> p t o", o=1).to_broadcast([P, n, w])

            def d1(u, t, G, n):
                dve.wait_ge(tail_ready, 2 * NB + u + 1)
                ev = G[:, :, 4 * D:4 * D + 2]
                dve.tensor_scalar(V[:, 0:n, 0:2], ev, ALPHA, None, ALU.mult)
                dve.drain()
                dve.tensor_tensor(V[:, 0:n, 0:2], V[:, 0:n, 0:2], ev, ALU.max)
                dve.drain()
                dve.tensor_tensor(V[:, 0:n, 0:2], V[:, 0:n, 0:2], pen[:, t, :], ALU.add)
                dve.memset(V[:, 0:n, 2:3], NEG_INF)
                dve.drain()
                dve.tensor_reduce(sm[:, 0, 0:n], V[:, 0:n, :], AX_X, ALU.max)
                dve.drain()
                dve.tensor_tensor(V[:, 0:n, :], V[:, 0:n, :], last_dim(sm[:, 0, 0:n], n, 3), ALU.subtract).then_inc(v_ready, 1)

            def d2(u, t, n):
                dve.wait_ge(e_ready, u + 1)
                dve.tensor_tensor(V[:, 0:n, :], E[:, 0:n, :], cnt[:, t, :], ALU.mult)
                dve.drain()
                dve.tensor_reduce(sm[:, 1, 0:n], V[:, 0:n, :], AX_X, ALU.add)
                dve.drain()
                dve.reciprocal(sm[:, 2, 0:n], sm[:, 1, 0:n])
                dve.drain()
                dve.tensor_tensor(pr[:, 0:n, :], E[:, 0:n, 0:2], last_dim(sm[:, 2, 0:n], n, 2), ALU.mult).then_inc(p_ready, 1)

            def d3(u, G, n, below):
                dve.wait_ge(t_ready, u + 1)
                if below:
                    dve.scalar_tensor_tensor(T1[:, 0, :], U1[:, G3:2 * G3], pr[:, 0, 1:2], T1[:, 0, :], ALU.mult, ALU.add)
                    dve.drain()
                dve.tensor_tensor(T1[:, 0:n, 0:2 * D], T1[:, 0:n, 0:2 * D], G[:, :, NODE + D:NODE + 3 * D], ALU.add).then_inc(g_ready, 1)
                dve.tensor_tensor(T1[:, 0:n, 2 * D:G3], T1[:, 0:n, 2 * D:G3],
                                  b_in_sb[:].rearrange("p (o d) -> p o d", o=1).to_broadcast([P, n, D]), ALU.add)

            def d4(u, G, n):
                dve.wait_ge(r_ready, u + 1)
                for k, hn in ((0, G[:, :, 0:D]), (1, G[:, :, NODE:NODE + D])):
                    dve.scalar_tensor_tensor(RH[:, k, 0:n, :], TH[:, k, 0:n, 0:D], 1.0, hn, ALU.add, ALU.mult)
                dve.drain()
                dve.scalar_tensor_tensor(PN[:, 1, 0:n, :], RH[:, 1, 0:n, :], 0.5, T1[:, 0:n, 2 * D:G3], ALU.mult, ALU.add)
                dve.scalar_tensor_tensor(PN[:, 0, 0:n, :], RH[:, 0, 0:n, :], 0.5, G[:, :, 3 * D:4 * D], ALU.mult, ALU.add)\
                    .then_inc(pn_ready, 1)

            def d5(u, t, n):
                dve.wait_ge(n_ready, u + 1)
                for k in range(2):
                    dve.tensor_tensor(OO[:, k, 0:n, :], H3[:, t, :], NN[:, k, 0:n, :], ALU.subtract)
                dve.drain()
                for k in range(2):
                    dve.scalar_tensor_tensor(OO[:, k, 0:n, :], TH[:, k, 0:n, D:2 * D], 1.0, OO[:, k, 0:n, :], ALU.add, ALU.mult)

            def d6(t, n):
                dve.drain()
                dve.tensor_tensor(OO[:, 0, 0:n, :], OO[:, 0, 0:n, :], OO[:, 1, 0:n, :], ALU.add)
                dve.tensor_tensor(NN[:, 0, 0:n, :], NN[:, 0, 0:n, :], NN[:, 1, 0:n, :], ALU.add)
                dve.drain()
                dve.scalar_tensor_tensor(RH[:, 0, 0:n, :], OO[:, 0, 0:n, :], 0.5, NN[:, 0, 0:n, :], ALU.mult, ALU.add)
                dve.drain()
                dve.tensor_tensor(RH[:, 1, 0:n, :], RH[:, 0, 0:n, :], last_dim(dN[:, t], n, D), ALU.mult)
                dve.drain()
                dve.tensor_tensor(X[:, t, :], X[:, t, :], RH[:, 1, 0:n, :], ALU.add).then_inc(out_ready, n)

            def tail3_step(b, s, below):
                if below:
                    it, k = divmod(s - 2, 3)
                    if not 0 <= it < IT:
                        return
                    u, t, G, n = b * IT + it, bass.ds(b * IT + it, 1), G1, 1
                else:
                    if s not in (5, 7, 9, 11, 13):
                        return
                    k, u, t, G, n = (s - 5) // 2, b, bass.ds(b * IT, IT), G4, IT
                if k == 0:
                    d1(u, t, G, n)
                if k == 1:
                    d2(u, t, n)
                    d3(u, G, n, below)
                if k == 2:
                    d4(u, G, n)
                if k == (2 if below else 3):
                    d5(u, t, n)
                if k == (2 if below else 4):
                    d6(t, n)

            def pass_block(p, below=False):
                def body(b, first, last):
                    for s in range(NS):
                        if p == 0 and first and s < BOTH:
                            if s % SQ == 0:
                                dve.wait_ge(nat_loaded[s // SQ], 16)
                        elif p == 0:
                            out_odd(b, s)
                        if p == 0 and first and (g := s // SQ + 1) < RT // LG:
                            if s % SQ == 0:
                                first_norm(g)
                            if s % SQ == 2:
                                second_norm(g)
                        if p < 2 and not first and s in TAIL_STEPS:
                            (tail1_step, tail2_step)[p](b - 1, TAIL_STEPS.index(s))
                        if p == 0:
                            count_above(b, s)
                            if s == NS - 1:
                                take_counts(b)
                        if p == 2:
                            if s == 0 and not first:
                                save3(b - 1, below)
                            ahead = 0 if below else 2
                            if s == (6 if first and not below else 1):
                                own_terms(b, below)
                            if not (last and s + ahead >= NS) and not (first and s + ahead < 2 * ahead):
                                mask(b, s + ahead, below)
                            if not first:
                                tail3_step(b - 1, s, below)
                return body

            def first_norm(g):
                t = slice(g * LG, (g + 1) * LG)
                dve.wait_ge(x_loaded[g], 16)
                norm_a(X[:, t, :], LG)
                norm_b(H01[:, t, 0:D], LG, 2 * g)
                dve.drain()
                dve.scalar_tensor_tensor(X[:, t, :], H01[:, t, 0:D], -B_CONST, X[:, t, :], ALU.mult, ALU.add)

            def second_norm(g):
                t = slice(g * LG, (g + 1) * LG)
                dve.drain()
                norm_a(X[:, t, :], LG)
                norm_b(H01[:, t, D:2 * D], LG, 2 * g + 1).then_inc(h_ready, 1)

            def take_products():
                dve.wait_ge(prod_made, 1)
                for w, k in ((we1_sb, 0), (we2_sb, 1)):
                    dve.tensor_copy(w[:, G3:G3 + 1], PS[:, TAIL2, k:k + 1])
                    dve.tensor_copy(w[:, G3 + 1:EV], PS[:, TAIL2, 1 - k:2 - k])
                dve.tensor_copy(v2_sb[:], PS[:, TAIL2, 2:2 + G3])
                dve.tensor_copy(diag_rows[:], PS[0:RT, TAIL2, 256:256 + P]).then_inc(diag_turned, 1)

            def count_rows():
                dve.drain()
                dve.wait_ge(w_loaded, 16 * N_LOADS)
                dve.tensor_scalar(dsign[:, 0, :], dN[:], 0.0, None, ALU.is_gt)
                dve.tensor_scalar(dsign[:, 1, :], dN[:], 0.0, None, ALU.is_lt)
                dve.tensor_tensor(sgn_n[:], pos_n[:], sgn_n[:], ALU.subtract)
                dve.drain()
                dve.tensor_reduce(below_p[:], sgn_n[:], AX_X, ALU.add).then_inc(below_counted, 1)
                dve.tensor_tensor(cnt[:, :, 0], pos_n[:], dsign[:, 0, :], ALU.subtract)
                dve.tensor_tensor(cnt[:, :, 1], sgn_n[:], dsign[:, 1, :], ALU.subtract)
                dve.drain()
                dve.tensor_tensor(sgn_n[:], cnt[:, :, 0], cnt[:, :, 1], ALU.add)
                dve.tensor_scalar(pen[:], cnt[:, :, 0:2], 0.0, ABSENT, ALU.is_equal, ALU.mult)
                dve.drain()
                dve.tensor_scalar(cnt[:, :, 2], sgn_n[:], -1.0, float(N), ALU.mult, ALU.add)

            def take_below():
                dve.tensor_scalar(any_below[:], PS[0:1, TAIL2, 508:509], 0.0, None, ALU.not_equal).then_inc(any_below_ready, 1)

            dve.memset(eps_sb[:], EPS)
            dve.memset(ones[:], 1.0)
            dve.memset(hT[:], 1.0)
            dve.memset(V[:], NEG_INF).then_inc(consts_made, 1)
            first_norm(0)
            second_norm(0)
            over_blocks(dve, pass_block(0), True)
            for k in range(len(TAIL_STEPS)):
                tail1_step(NB - 1, k)
            count_rows()
            take_products()
            take_below()
            all_spilled(dve)
            over_blocks(dve, pass_block(1), False)
            dve.memset(own, 0.0)

            def pass3(below):
                if not below:
                    for s in range(4):
                        mask(0, s, below)
                for k in range(len(TAIL_STEPS)):
                    tail2_step(NB - 1, k)
                over_blocks(dve, pass_block(2, below), True)
                save3(NB - 1, below)
                for s in range(NS):
                    tail3_step(NB - 1, s, below)

            either_way(dve, pass3)


def kernel(**inputs):
    import concourse.bacc as bacc
    from concourse.bass_utils import run_bass_kernel_spmd

    a = {k: np.asarray(v) for k, v in inputs.items()}
    D = a["x"].shape[1]
    f32 = np.float32

    bd1 = np.zeros((2 * D, 2 * D), f32)
    bd1[:D, :D] = np.eye(D, dtype=f32)
    bd1[D:, D:] = a["L1_gnn_weight"]
    twice = lambda w: np.concatenate([w, w], axis=0)
    wih_e = a["L3_gnn_w_ih_e"]
    haug = np.zeros((D + 2, 7 * D + 2), f32)
    for base, k, cols in ((0, "e", "rzn"), (4 * D + 2, "n", "rz")):
        whh, bih, bhh = a[f"L3_gnn_w_hh_{k}"], a[f"L3_gnn_b_ih_{k}"], a[f"L3_gnn_b_hh_{k}"]
        haug[:D, base:base + D] = whh[2 * D:].T
        haug[D + 1, base:base + D] = bhh[2 * D:]
        haug[:D, base + D:base + 3 * D] = whh[:2 * D].T
        haug[D, base + D:base + 3 * D] = bih[:2 * D]
        haug[D + 1, base + D:base + 3 * D] = bhh[:2 * D]
        if "n" in cols:
            haug[D, base + 3 * D:base + 4 * D] = bih[2 * D:]
    arrays = {
        "x": a["x"], "adj": a["adj"], "bd1": bd1, "w2s": twice(a["L2_gnn_W"]),
        "b2": a["L2_gnn_b"].reshape(1, D),
        "wgat_t2": np.concatenate([a["L3_gnn_W_gat"].T, a["L3_gnn_W_gat"].T], axis=1),
        "a2": np.concatenate([a["L3_gnn_a_gat"][:D], a["L3_gnn_a_gat"][D:]], axis=1),
        "wih_n_t": a["L3_gnn_w_ih_n"].T,
        "b_in": a["L3_gnn_b_ih_n"][2 * D:].reshape(1, D),
        "we1": twice(wih_e[:, :D].T), "we2": twice(wih_e[:, D:].T), "haug": haug,
    }
    nc = bacc.Bacc("TRN2", target_bir_lowering=False, num_devices=1)
    args, maps = [], {}
    for name, v in arrays.items():
        v = np.ascontiguousarray(v)
        maps[f"in_{name}"] = v
        args.append(nc.dram_tensor(f"in_{name}", v.shape, mybir.dt.from_np(v.dtype), kind="ExternalInput").ap())
    out = nc.dram_tensor("out", a["x"].shape, F32, kind="ExternalOutput").ap()
    gnn_stack(nc, *args, out)
    r = run_bass_kernel_spmd(nc, [maps], core_ids=[0])
    return r.results[0]["out"]
```
